# Optimizing a Trainium2 kernel written in Bass

```python
import numpy as np
import jax
import jax.numpy as jnp

def _softmax(x, axis=-1):
    return jax.nn.softmax(x, axis=axis)

def _gelu(x):
    return jax.nn.gelu(x, approximate=True)

def _silu(x):
    return jax.nn.silu(x)

def _sigmoid(x):
    return jax.nn.sigmoid(x)

def _layernorm(x, axis=-1, eps=1e-05):
    m = jnp.mean(x, axis=axis, keepdims=True)
    v = jnp.var(x, axis=axis, keepdims=True)
    return (x - m) / jnp.sqrt(v + eps)

def _scatter_add(tgt, idx, src, axis=0):
    return tgt.at[idx].add(src)

def _segment_sum(src, seg, n):
    return jax.ops.segment_sum(src, seg, n)
kernel_name = 'mk_macaron_d1_jaxref_r8_05766b'

def setup_inputs(seed: int=0):
    np.random.seed(seed)
    _w = jnp.asarray

    def _L0_attn_setup():
        import jax, jax.numpy as jnp
        import numpy as np
        import math
        B, S, D = (4, 256, 128)
        H, KV = (16, 4)
        HD = D // H
        GROUPS = H // KV

        def _alibi_slopes(n):
            start = 2.0 ** (-2.0 ** (-(math.log2(n) - 3)))
            return np.array([start * start ** i for i in range(n)], dtype=np.float32)
        key = jax.random.key(seed)
        ks = jax.random.split(key, 5)
        sc = 0.02
        return {'x': jax.random.normal(ks[0], (B, S, D), jnp.float32), 'Wq': jax.random.normal(ks[1], (D, H * HD), jnp.float32) * sc, 'Wk': jax.random.normal(ks[2], (D, KV * HD), jnp.float32) * sc, 'Wv': jax.random.normal(ks[3], (D, KV * HD), jnp.float32) * sc, 'Wo': jax.random.normal(ks[4], (H * HD, D), jnp.float32) * sc}
    _L0_attn_in = _L0_attn_setup()

    def _L0_ffn_setup():
        import jax, jax.numpy as jnp
        import numpy as np
        DIM = 128
        HEADS = 16
        HD = DIM // HEADS
        M = 32
        E = 4
        K = 2
        HID = 256
        MID = 256
        LB = 0.01
        EPS = 1.1920929e-07

        def _rms(x, w):
            return x * jax.lax.rsqrt(jnp.mean(x * x, axis=-1, keepdims=True) + EPS) * w

        def _gelu(x):
            return jax.nn.gelu(x, approximate=False)
        key = jax.random.key(seed)
        ks = jax.random.split(key, 20)
        d = DIM
        w = lambda k, s: jax.random.normal(k, s, jnp.float32) * 0.02
        return {'x': jax.random.normal(ks[0], (4, 128, d), jnp.float32), 'n1_w': jnp.ones((d,), jnp.float32), 'n2_w': jnp.ones((d,), jnp.float32), 'wq': w(ks[1], (d, d)), 'wk': w(ks[2], (d, d)), 'wv': w(ks[3], (d, d)), 'wo': w(ks[4], (d, d)), 'qn_w': jnp.ones((HD,), jnp.float32), 'kn_w': jnp.ones((HD,), jnp.float32), 'gate_w': w(ks[5], (E, d)), 'e0_up': w(ks[6], (HID, d)), 'e0_down': w(ks[7], (d, HID)), 'e1_w1': w(ks[8], (HID, d)), 'e1_w2': w(ks[9], (HID, d)), 'e1_down': w(ks[10], (d, HID)), 'e2_l1': w(ks[11], (MID, d)), 'e2_l2': w(ks[12], (HID, MID)), 'e2_l3': w(ks[13], (MID, HID)), 'e2_l4': w(ks[14], (d, MID)), 'e3_down': w(ks[15], (d, d)), 'e3_up': w(ks[16], (HID, d)), 'e3_out': w(ks[17], (d, HID))}
    _L0_ffn_in = _L0_ffn_setup()
    _d = {'L0_attn_x': _L0_attn_in['x'], 'L0_attn_Wq': _L0_attn_in['Wq'], 'L0_attn_Wk': _L0_attn_in['Wk'], 'L0_attn_Wv': _L0_attn_in['Wv'], 'L0_attn_Wo': _L0_attn_in['Wo'], 'L0_ffn_n1_w': _L0_ffn_in['n1_w'], 'L0_ffn_n2_w': _L0_ffn_in['n2_w'], 'L0_ffn_wq': _L0_ffn_in['wq'], 'L0_ffn_wk': _L0_ffn_in['wk'], 'L0_ffn_wv': _L0_ffn_in['wv'], 'L0_ffn_wo': _L0_ffn_in['wo'], 'L0_ffn_qn_w': _L0_ffn_in['qn_w'], 'L0_ffn_kn_w': _L0_ffn_in['kn_w'], 'L0_ffn_gate_w': _L0_ffn_in['gate_w'], 'L0_ffn_e0_up': _L0_ffn_in['e0_up'], 'L0_ffn_e0_down': _L0_ffn_in['e0_down'], 'L0_ffn_e1_w1': _L0_ffn_in['e1_w1'], 'L0_ffn_e1_w2': _L0_ffn_in['e1_w2'], 'L0_ffn_e1_down': _L0_ffn_in['e1_down'], 'L0_ffn_e2_l1': _L0_ffn_in['e2_l1'], 'L0_ffn_e2_l2': _L0_ffn_in['e2_l2'], 'L0_ffn_e2_l3': _L0_ffn_in['e2_l3'], 'L0_ffn_e2_l4': _L0_ffn_in['e2_l4'], 'L0_ffn_e3_down': _L0_ffn_in['e3_down'], 'L0_ffn_e3_up': _L0_ffn_in['e3_up'], 'L0_ffn_e3_out': _L0_ffn_in['e3_out']}
    _x0 = _d['L0_attn_x']
    _d['L0_attn_x'] = jax.random.normal(jax.random.fold_in(jax.random.key(seed), 1), (4, 1024, 128), dtype=_x0.dtype)
    del _x0
    return _d

def reference(L0_attn_x, L0_attn_Wq, L0_attn_Wk, L0_attn_Wv, L0_attn_Wo, L0_ffn_n1_w, L0_ffn_n2_w, L0_ffn_wq, L0_ffn_wk, L0_ffn_wv, L0_ffn_wo, L0_ffn_qn_w, L0_ffn_kn_w, L0_ffn_gate_w, L0_ffn_e0_up, L0_ffn_e0_down, L0_ffn_e1_w1, L0_ffn_e1_w2, L0_ffn_e1_down, L0_ffn_e2_l1, L0_ffn_e2_l2, L0_ffn_e2_l3, L0_ffn_e2_l4, L0_ffn_e3_down, L0_ffn_e3_up, L0_ffn_e3_out):

    def _L0_attn_ref(x, Wq, Wk, Wv, Wo):
        import jax, jax.numpy as jnp
        import numpy as np
        import math
        B, S, D = (4, 256, 128)
        H, KV = (16, 4)
        HD = D // H
        GROUPS = H // KV

        def _alibi_slopes(n):
            start = 2.0 ** (-2.0 ** (-(math.log2(n) - 3)))
            return np.array([start * start ** i for i in range(n)], dtype=np.float32)
        b, s, _ = x.shape
        scale = HD ** (-0.5)
        q = (x @ Wq).reshape(b, s, H, HD).transpose(0, 2, 1, 3)
        k = (x @ Wk).reshape(b, s, KV, HD).transpose(0, 2, 1, 3)
        v = (x @ Wv).reshape(b, s, KV, HD).transpose(0, 2, 1, 3)
        k = jnp.repeat(k, GROUPS, axis=1)
        v = jnp.repeat(v, GROUPS, axis=1)
        attn = jnp.einsum('bhqd,bhkd->bhqk', q, k) * scale
        slopes = jnp.asarray(_alibi_slopes(H))
        pos = jnp.arange(s, dtype=jnp.float32)
        rel = pos[None, :] - pos[:, None]
        attn = attn + slopes[None, :, None, None] * rel[None, None, :, :]
        attn = jax.nn.softmax(attn, axis=-1)
        out = jnp.einsum('bhqk,bhkd->bhqd', attn, v)
        out = out.transpose(0, 2, 1, 3).reshape(b, s, H * HD)
        return out @ Wo

    def _L0_ffn_ref(x, n1_w, n2_w, wq, wk, wv, wo, qn_w, kn_w, gate_w, e0_up, e0_down, e1_w1, e1_w2, e1_down, e2_l1, e2_l2, e2_l3, e2_l4, e3_down, e3_up, e3_out):
        import jax, jax.numpy as jnp
        import numpy as np
        DIM = 128
        HEADS = 16
        HD = DIM // HEADS
        M = 32
        E = 4
        K = 2
        HID = 256
        MID = 256
        LB = 0.01
        EPS = 1.1920929e-07

        def _rms(x, w):
            return x * jax.lax.rsqrt(jnp.mean(x * x, axis=-1, keepdims=True) + EPS) * w

        def _gelu(x):
            return jax.nn.gelu(x, approximate=False)
        B, T, C = x.shape
        h = _rms(x, n1_w)
        heads = lambda w_: (h @ w_.T).reshape(B, T, HEADS, HD).transpose(0, 2, 1, 3)
        q = _rms(heads(wq), qn_w)
        k = _rms(heads(wk), kn_w)
        v = heads(wv)
        scores = jnp.einsum('bhqd,bhkd->bhqk', q, k) * HD ** (-0.5)
        causal = jnp.tril(jnp.ones((T, T), bool))
        scores = jnp.where(causal[None, None], scores, -jnp.inf)
        attn = jax.nn.softmax(scores, axis=-1)
        ao = jnp.einsum('bhqk,bhkd->bhqd', attn, v).transpose(0, 2, 1, 3).reshape(B, T, C) @ wo.T
        ao = ao.at[:, :, :M].set(0.0)
        x = x + ao
        xf = _rms(x, n2_w).reshape(-1, C)
        N = xf.shape[0]
        logits = jnp.nan_to_num(xf @ gate_w.T)
        probs = jax.nn.softmax(logits, axis=-1)
        topv, topi = jax.lax.top_k(probs, K)
        topv = topv / (topv.sum(-1, keepdims=True) + 1e-08)
        wts = jnp.zeros((N, E), x.dtype).at[jnp.arange(N)[:, None], topi].add(topv)
        o0 = _gelu(xf @ e0_up.T) @ e0_down.T
        o1 = jax.nn.silu(xf @ e1_w1.T) * (xf @ e1_w2.T) @ e1_down.T
        o2 = _gelu(_gelu(_gelu(xf @ e2_l1.T) @ e2_l2.T) @ e2_l3.T) @ e2_l4.T
        o3 = _gelu(_gelu(xf @ e3_down.T) @ e3_up.T) @ e3_out.T
        moe = wts[:, 0:1] * o0 + wts[:, 1:2] * o1 + wts[:, 2:3] * o2 + wts[:, 3:4] * o3
        moe = moe.reshape(B, T, C).at[:, :, :M].set(0.0)
        return x + moe
    x = L0_attn_x
    x = x + 0.5 * _L0_ffn_ref(_layernorm(x, axis=-1), L0_ffn_n1_w, L0_ffn_n2_w, L0_ffn_wq, L0_ffn_wk, L0_ffn_wv, L0_ffn_wo, L0_ffn_qn_w, L0_ffn_kn_w, L0_ffn_gate_w, L0_ffn_e0_up, L0_ffn_e0_down, L0_ffn_e1_w1, L0_ffn_e1_w2, L0_ffn_e1_down, L0_ffn_e2_l1, L0_ffn_e2_l2, L0_ffn_e2_l3, L0_ffn_e2_l4, L0_ffn_e3_down, L0_ffn_e3_up, L0_ffn_e3_out)
    x = x + _L0_attn_ref(_layernorm(x, axis=-1), L0_attn_Wq, L0_attn_Wk, L0_attn_Wv, L0_attn_Wo)
    x = x + 0.5 * _L0_ffn_ref(_layernorm(x, axis=-1), L0_ffn_n1_w, L0_ffn_n2_w, L0_ffn_wq, L0_ffn_wk, L0_ffn_wv, L0_ffn_wo, L0_ffn_qn_w, L0_ffn_kn_w, L0_ffn_gate_w, L0_ffn_e0_up, L0_ffn_e0_down, L0_ffn_e1_w1, L0_ffn_e1_w2, L0_ffn_e1_down, L0_ffn_e2_l1, L0_ffn_e2_l2, L0_ffn_e2_l3, L0_ffn_e2_l4, L0_ffn_e3_down, L0_ffn_e3_up, L0_ffn_e3_out)
    return x

_drawn_inputs = setup_inputs


def setup_inputs(seed=0):
    import zlib

    import numpy as np

    out = dict(_drawn_inputs(seed))
    spreads = {'L0_ffn_n1_w': (1.0, 0.6),
     'L0_ffn_n2_w': (1.0, 0.6),
     'L0_ffn_qn_w': (1.0, 0.6),
     'L0_ffn_kn_w': (1.0, 0.6)}
    factors = {'L0_attn_Wq': 8.0,
     'L0_attn_Wk': 8.0,
     'L0_attn_Wv': 6.435,
     'L0_attn_Wo': 6.767,
     'L0_ffn_wq': 8.0,
     'L0_ffn_wk': 8.0,
     'L0_ffn_wv': 8.0,
     'L0_ffn_wo': 8.0,
     'L0_ffn_gate_w': 8.0,
     'L0_ffn_e0_up': 8.0,
     'L0_ffn_e0_down': 8.0,
     'L0_ffn_e1_w1': 8.0,
     'L0_ffn_e1_w2': 8.0,
     'L0_ffn_e1_down': 8.0,
     'L0_ffn_e2_l1': 8.0,
     'L0_ffn_e2_l2': 8.0,
     'L0_ffn_e2_l3': 8.0,
     'L0_ffn_e2_l4': 8.0,
     'L0_ffn_e3_down': 8.0,
     'L0_ffn_e3_up': 8.0,
     'L0_ffn_e3_out': 8.0}
    for name, (base, spread) in spreads.items():
        noise = np.random.default_rng([zlib.crc32(name.encode()), seed]).standard_normal(out[name].shape)
        drawn = base * np.exp(spread * noise) if base else spread * noise
        out[name] = jnp.asarray(drawn.astype(out[name].dtype))
    for name, factor in factors.items():
        out[name] = (out[name] * factor).astype(out[name].dtype)
    return out
```

```python
import math
from contextlib import ExitStack

import numpy as np
import concourse.bass as bass
from concourse import mybir

FP32 = mybir.dt.float32
BF16 = mybir.dt.bfloat16
I32 = mybir.dt.int32
ALU = mybir.AluOpType
ACT = mybir.ActivationFunctionType
AXX = mybir.AxisListType.X

B, S, D = 4, 1024, 128
P = 128
T = S // P
H, HD = 16, 8
KV = 4
G = H // 4
BANK = 512
HALVES = S // BANK
HB = P // HD
FFN_HID = 256
KEEP0 = 32
OUTW = D - KEEP0
E = 4
LN_EPS = 1e-5
RMS_EPS = 1.1920929e-07
SCALE = float(np.float32(HD ** -0.5))
FMAX = float(np.finfo(np.float32).max)
MASKED = -1.0e30

QPART = (0, 0, 0, 1, 1, 2)
KPART = (0, 1, 2, 0, 1, 0)
HROWS = 64
EXTRA = HD * len(QPART)
NC_ROWS = 3
NEXTRA = HROWS - EXTRA


def f32_parts(v):
    out, rest = [], np.float32(v)
    for _ in range(3):
        bits = np.array(rest, np.float32).view(np.uint32).astype(np.uint64)
        r = ((bits + 0x7FFF + ((bits >> 16) & 1)) >> 16 << 16).astype(np.uint32).view(np.float32)
        out.append(np.float32(r))
        rest = np.float32(rest - np.float32(r))
    return out


def additive_rows():
    key = np.zeros((NEXTRA, S), np.float32)
    key[0:NC_ROWS] = 1.0
    rel = np.arange(S) - (S - 1)
    low = rel % 4
    for n in range(3):
        key[NC_ROWS + 2 * n] = rel - low
        key[NC_ROWS + 2 * n + 1] = low
    query = np.zeros((2, NEXTRA, H, S), np.float32)
    start = 2.0 ** (-2.0 ** (-(math.log2(H) - 3)))
    for h in range(H):
        for n, part in enumerate(f32_parts(np.float32(start * start ** h))):
            query[1, NC_ROWS + 2 * n, h] = part
            query[1, NC_ROWS + 2 * n + 1, h] = part
    return key, query


def columns(parts):
    at, out = 0, {}
    for name, width in parts:
        out[name] = at
        at += width
    return out, at


WPARTS = [("wq", D), ("wk", D), ("wv", D),
          ("gate", E), ("e0u", 256), ("e1g", 256), ("e1u", 256), ("e2a", 256), ("e3a", 128),
          ("wo", D), ("e2b", 512), ("e2c", 512), ("e3b", 256),
          ("d0", 256), ("d1", 256), ("d2", 256), ("d3", 256),
          ("aq", D), ("ak", D), ("av", D), ("ao", D)]
WAT, WCOLS = columns(WPARTS)




def macaron_kernel(nc, x, weights, vectors, key_rows, query_rows, out):
    ctx = ExitStack()
    with ctx:
        def sb(name, shape, dt):
            return ctx.enter_context(nc.sbuf_tensor(name, shape, dt))

        def sem(name):
            return ctx.enter_context(nc.semaphore(name))

        X = sb("X", [P, B * T * D], FP32)
        U = sb("U", [P, T, D], FP32)
        W = sb("W", [P, WCOLS], FP32)
        VEC = sb("VEC", [P, 4], FP32)
        ident = sb("ident", [P, P], FP32)
        identb = sb("identb", [P, P], BF16)
        negmask = sb("negmask", [P, P], BF16)
        headsum = sb("headsum", [P, P], FP32)
        QS = sb("QS", [P, H // 2, S], BF16)
        KZ = sb("KZ", [P, H, S], BF16)
        V = sb("V", [P, T, H, 32], FP32)
        hT = sb("hT", [P, S], FP32)
        QK = sb("QK", [P, 2, S], FP32)
        SQ = sb("SQ", [P, 2, S], FP32)
        PARTS = sb("PARTS", [P, 2, 3, S], BF16)
        EXPS = sb("EXPS", [P, 2, 4, S], FP32)
        NM = sb("NM", [P, 2, T, 4], FP32)
        NR = sb("NR", [P, T, 4], FP32)
        CT = sb("CT", [P, 2, T, NC_ROWS, 4], BF16)
        CTS = sb("CTS", [NC_ROWS * 4, 2, S], BF16)
        OT = sb("OT", [P, S], FP32)
        RD = sb("RD", [P, T, 4], FP32)
        AO = sb("AO", [P, T, D], FP32)
        BST = sb("BST", [P, T, 6], FP32)
        MV = sb("MV", [P, T, 2], FP32)
        RSTD = sb("RSTD", [P, T], FP32)
        VAR2 = sb("VAR2", [P, T], FP32)
        R1 = sb("R1", [P, T], FP32)
        R2 = sb("R2", [P, 4], FP32)
        EPS = sb("EPS", [P, 4], FP32)
        RT = sb("RT", [P, 12, 4, E], FP32)
        RS = sb("RS", [P, 4, 4], FP32)
        CMP = sb("CMP", [P, 4, E, E], FP32)
        WD = sb("WD", [P, 2, E, OUTW], FP32)
        WS = sb("WS", [P, 2, OUTW], FP32)
        HID = EXPS[:, :, :, :].rearrange("p a b (c n) -> p (a b c) n", n=BANK)
        H0, H1, A1, A2, A3, B2 = (HID[:, 2 * i:2 * i + 2, :] for i in range(6))
        TH, B1, YT = HID[:, 12:14, :], HID[:, 14, :], HID[:, 15, :]
        SCR = nc.dram_tensor("scratch_parts", [2, 3, P, S], BF16).ap()

        PS = ctx.enter_context(nc.psum_tensor("PS", [P, 8 * BANK], FP32))

        def bank(n, width=BANK):
            return PS[:, n * BANK:n * BANK + width]

        def wcol(name, a=0, b=None):
            return W[:, WAT[name] + a:WAT[name] + b]

        loaded, zeroed, drawn, scaled = sem("loaded"), sem("zeroed"), sem("drawn"), sem("scaled")

        def clear(sems):
            for s in sems.values():
                nc.sync.sem_clear(s)
            nc.all_engine_barrier()

        with nc.Block() as block:
            @block.sync
            def _(sp):
                sp.dma_start(X[:, :].rearrange("p (n d) -> p n d", d=D), x.rearrange("b (t p) d -> p (b t) d", p=P))\
                  .then_inc(loaded, 16)
                sp.dma_start(VEC[:, :], vectors).then_inc(loaded, 16)
                sp.dma_start(W[:, :], weights).then_inc(loaded, 16)
                sp.wait_ge(zeroed, 2)
                for e in range(2):
                    rows = slice(HROWS * e + EXTRA, HROWS * (e + 1))
                    sp.dma_start(KZ[rows, :, :].rearrange("p (q e) t -> p e q t", e=2)[:, e], key_rows)\
                      .then_inc(loaded, 16)
                sp.wait_ge(loaded, 16 * 5)

            @block.vector
            def _(dve):
                dve.memset(V[:, :, :, :], 0.0).then_inc(zeroed, 1)
                dve.memset(KZ[:, :, :].bitcast(I32), 0).then_inc(zeroed, 1)
                dve.wait_ge(zeroed, 2)
                dve.memset(V[:, :, :, HD:HD + 1], 1.0)
                dve.memset(CMP[:, :, :, :], 0.0)
                for n, value in enumerate((LN_EPS, RMS_EPS, 0.0)):
                    dve.memset(EPS[:, n:n + 1], value)
                dve.wait_ge(loaded, 16 * 5)
                for lo, hi, n in ((WAT["wq"], WAT["gate"], 0), (WAT["gate"], WAT["wo"], 1)):
                    dve.tensor_scalar(W[:, lo:hi], W[:, lo:hi], VEC[:, n:n + 1], None, ALU.mult)
                dve.tensor_scalar(VEC[:, 2:3], VEC[:, 2:3], SCALE, None, ALU.mult)

            @block.gpsimd
            def _(pool):
                pool.memset(ident[:, :], 0.0).then_inc(drawn, 1)
                pool.memset(identb[:, :], 0.0).then_inc(drawn, 1)
                pool.memset(negmask[:, :], 0.0).then_inc(drawn, 1)
                pool.memset(headsum[:, :], 1.0).then_inc(drawn, 1)
                pool.wait_ge(drawn, 4)
                for m in (ident, identb):
                    pool.affine_select(out=m[:, :], in_=m[:, :], compare_op=ALU.not_equal, fill=1.0, base=0,
                                       pattern=[[-1, P]], channel_multiplier=1).then_inc(drawn, 1)
                pool.affine_select(out=negmask[:, :], in_=negmask[:, :], compare_op=ALU.is_ge, fill=MASKED, base=0,
                                   pattern=[[-1, P]], channel_multiplier=1).then_inc(drawn, 1)
                pool.affine_select(out=headsum[:, :], in_=headsum[:, :], compare_op=ALU.is_ge, fill=0.0, base=0,
                                   pattern=[[-HD, HB], [0, HD]], channel_multiplier=1).then_inc(drawn, 1)
                pool.wait_ge(drawn, 8)
                pool.affine_select(out=headsum[:, :], in_=headsum[:, :], compare_op=ALU.is_ge, fill=0.0, base=HD - 1,
                                   pattern=[[HD, HB], [0, HD]], channel_multiplier=-1)

        PSEMS = ("p_chain", "stats", "sd", "rstd", "v2", "r1root", "u_ready", "hn_ready", "t_psum", "hT_ready",
                 "proj", "vproj", "v_ready", "squares", "head_sums", "roots", "qk_ready", "part0", "rest", "part1",
                 "part2", "q_scratch", "k_scratch", "stacked")
        ps = {n: sem(n) for n in PSEMS}
        N_STACK = 2 + 2 * 2 * len(QPART)

        def prep(b, ffn):
            wq, wk, wv = ("wq", "wk", "wv") if ffn else ("aq", "ak", "av")
            turns = [(i % 2, i // 2) for i in range(4)]

            def cols(half):
                return slice(half * BANK, (half + 1) * BANK)

            with nc.Block() as block:
                @block.vector
                def _(dve):
                    chain = [0]

                    def link(ins):
                        chain[0] += 1
                        ins.then_inc(ps["p_chain"], 1)
                        dve.wait_ge(ps["p_chain"], chain[0])

                    for t in range(T):
                        last = dve.bn_stats(BST[:, t, :], X[:, bass.ts(b * T + t, D)])
                    link(last)
                    for t in range(T):
                        last = dve.bn_aggr(MV[:, t, :], BST[:, t, :])
                    last.then_inc(ps["stats"], 1)
                    dve.wait_ge(ps["sd"], 1)
                    link(dve.reciprocal(RSTD[:, :], RSTD[:, :]))
                    if ffn:
                        link(dve.tensor_tensor(VAR2[:, :], MV[:, :, 1], RSTD[:, :], ALU.mult))
                        dve.tensor_tensor(VAR2[:, :], VAR2[:, :], RSTD[:, :], ALU.mult).then_inc(ps["v2"], 1)
                    for t in range(T):
                        dve.tensor_scalar(U[:, t, :], X[:, bass.ts(b * T + t, D)], MV[:, t, 0:1], RSTD[:, t:t + 1],
                                          ALU.subtract, ALU.mult).then_inc(ps["u_ready"], 1)
                        if ffn and t == 1:
                            dve.wait_ge(ps["r1root"], 1)
                            dve.reciprocal(R1[:, :], R1[:, :]).then_inc(ps["rstd"], 1)

                    def rest(i):
                        w, half = turns[i]
                        dve.wait_ge(ps["part0"], i + 1)
                        dve.tensor_tensor(SQ[:, w, cols(half)], QK[:, w, cols(half)], PARTS[:, w, 0, cols(half)],
                                          ALU.subtract).then_inc(ps["rest"], 1)

                    def last_part(i):
                        w, half = turns[i]
                        dve.wait_ge(ps["part1"], i + 1)
                        dve.tensor_tensor(PARTS[:, w, 2, cols(half)], SQ[:, w, cols(half)], PARTS[:, w, 1, cols(half)],
                                          ALU.subtract).then_inc(ps["part2"], 1)

                    for i in range(6):
                        if i < 4 and ffn:
                            w, half = turns[i]
                            dve.wait_ge(ps["roots"], i + 1)
                            link(dve.reciprocal(SQ[:, w, cols(half)], SQ[:, w, cols(half)]))
                            dve.scalar_tensor_tensor(QK[:, w, cols(half)], bank(2 + 2 * w + half), VEC[:, 2 + w:3 + w],
                                                     SQ[:, w, cols(half)], ALU.mult, ALU.mult).then_inc(ps["qk_ready"], 1)
                        if 1 <= i <= 4:
                            rest(i - 1)
                        if i >= 2:
                            last_part(i - 2)

                @block.scalar
                def _(act):
                    act.wait_ge(ps["stats"], 1)
                    act.activation(RSTD[:, :], MV[:, :, 1], ACT.Sqrt, bias=EPS[:, 0:1]).then_inc(ps["sd"], 1)
                    if ffn:
                        act.wait_ge(ps["v2"], 1)
                        act.activation(R1[:, :], VAR2[:, :], ACT.Sqrt, bias=EPS[:, 1:2]).then_inc(ps["r1root"], 1)
                        act.wait_ge(ps["rstd"], 1)
                        for t in range(T):
                            act.wait_ge(ps["u_ready"], t + 1)
                            act.activation(AO[:, t, :], U[:, t, :], ACT.Copy, scale=R1[:, t:t + 1])\
                               .then_inc(ps["hn_ready"], 1)
                    for half in range(HALVES):
                        act.wait_ge(ps["t_psum"], half + 1)
                        act.activation(hT[:, cols(half)], bank(half), ACT.Copy).then_inc(ps["hT_ready"], 1)
                    for i, (w, half) in enumerate(turns):
                        act.wait_ge(ps["proj"], i + 1)
                        if ffn:
                            act.activation(SQ[:, w, cols(half)], bank(2 + 2 * w + half), ACT.Square)\
                               .then_inc(ps["squares"], 1)
                        else:
                            act.activation(QK[:, w, cols(half)], bank(2 + 2 * w + half), ACT.Copy,
                                           scale=(SCALE if w == 0 else 1.0)).then_inc(ps["qk_ready"], 1)
                    if ffn:
                        for i, (w, half) in enumerate(turns):
                            act.wait_ge(ps["head_sums"], i + 1)
                            act.activation(SQ[:, w, cols(half)], bank(i % 2), ACT.Sqrt, bias=EPS[:, 1:2],
                                           scale=1.0 / HD).then_inc(ps["roots"], 1)
                    for half in range(HALVES):
                        act.wait_ge(ps["vproj"], half + 1)
                        act.activation(V[:, 4 * half:4 * half + 4, :, 0:HD],
                                       bank(6 + half).rearrange("p (t h d) -> p t h d", t=4, d=HD),
                                       ACT.Copy).then_inc(ps["v_ready"], 1)

                @block.gpsimd
                def _(pool):
                    def take(part, src, i, done):
                        w, half = turns[i]
                        pool.tensor_copy(PARTS[:, w, part, cols(half)], src[:, w, cols(half)]).then_inc(ps[done], 1)

                    for i in range(5):
                        if i < 4:
                            pool.wait_ge(ps["qk_ready"], i + 1)
                            take(0, QK, i, "part0")
                        if i >= 1:
                            pool.wait_ge(ps["rest"], i)
                            take(1, SQ, i - 1, "part1")

                @block.tensor
                def _(pe):
                    for t in range(T):
                        pe.wait_ge(ps["hn_ready" if ffn else "u_ready"], t + 1)
                        src = AO if ffn else U
                        last = pe.transpose(bank(t // 4)[:, (t % 4) * D:(t % 4 + 1) * D], src[:, t, :], ident[:, :])
                        if t % 4 == 3:
                            last.then_inc(ps["t_psum"], 1)
                    for i, (w, half) in enumerate(turns):
                        pe.wait_ge(ps["hT_ready"], half + 1)
                        pe.matmul(bank(2 + 2 * w + half), wcol((wq, wk)[w], 0, D), hT[:, cols(half)],
                                  start=True, stop=True).then_inc(ps["proj"], 1)
                    for t in range(T):
                        last = pe.matmul(bank(6 + t // 4)[:, (t % 4) * D:(t % 4 + 1) * D], hT[:, t * P:(t + 1) * P],
                                         wcol(wv, 0, D), start=True, stop=True)
                        if t % 4 == 3:
                            last.then_inc(ps["vproj"], 1)
                    if ffn:
                        for i, (w, half) in enumerate(turns):
                            pe.wait_ge(ps["squares"], i + 1)
                            if i >= 2:
                                pe.wait_ge(ps["roots"], i - 1)
                            pe.matmul(bank(i % 2), headsum[:, :], SQ[:, w, cols(half)], start=True, stop=True)\
                              .then_inc(ps["head_sums"], 1)

                @block.sync
                def _(sp):
                    scr = SCR.rearrange("w s (q e d) t -> w s e d q t", e=2, d=HD)
                    kz = KZ[:, :, :].rearrange("p (q e) t -> p e q t", e=2)
                    additive = query_rows[0 if ffn else 1].rearrange("r (q e) t -> e r q t", e=2)
                    for e in range(2):
                        sp.dma_start(QS[HROWS * e + EXTRA:HROWS * (e + 1), :, :], additive[e]).then_inc(ps["stacked"], 16)
                    for w in range(2):
                        scratch = ps["q_scratch" if w == 0 else "k_scratch"]
                        sp.wait_ge(ps["part2"], 3 + w)
                        sp.dma_start(SCR[w].rearrange("s p t -> p s t"), PARTS[:, w, :, :]).then_inc(scratch, 16)
                    for w in range(2):
                        sp.wait_ge(ps["q_scratch" if w == 0 else "k_scratch"], 16)
                        for s, part in enumerate((QPART, KPART)[w]):
                            for e in range(2):
                                rows = slice(HROWS * e + HD * s, HROWS * e + HD * (s + 1))
                                to = QS[rows, :, :] if w == 0 else kz[rows, e, :, :]
                                sp.dma_start(to, scr[w, part, e]).then_inc(ps["stacked"], 16)
                    sp.wait_ge(ps["stacked"], 16 * N_STACK)

            clear(ps)

        ASEMS = ("a_chain", "g_chain", "scores", "exp_done", "diag_done", "pv_done", "ring_full", "ring_free",
                 "split_done", "max_loaded", "o_evac")
        as_ = {n: sem(n) for n in ASEMS}

        def pieces(causal):
            out = []
            for kt in range(T):
                for half in range(HALVES):
                    lo = max(half * BANK, kt * P if causal else 0)
                    if lo < (half + 1) * BANK:
                        out.append((kt, half, lo, (half + 1) * BANK))
            return out

        def order(causal):
            steps = []
            maxima = [("max", j, qt) for j in range(4) for qt in (7, 0, 6, 1, 5, 2, 4, 3)]
            steps += [("max", 0, j, qt) for _, j, qt in maxima] + [("split", 0), ("turn", 0)]
            pcs = pieces(causal)
            n = 4 * len(pcs)
            for g in range(G):
                done, at = 0, 0
                for q, piece in enumerate(pcs):
                    for j in range(4):
                        steps.append(("score", g, j, piece))
                        at += 1
                        if g > 0 and at == 4:
                            steps.append(("evac", g - 1))
                        if g > 0 and at == 10:
                            steps.append(("out", g - 1))
                        if g + 1 < G:
                            while done < len(maxima) and done * (0.75 * n) < at * len(maxima):
                                steps.append(("max", g + 1) + maxima[done][1:])
                                done += 1
                                if done == len(maxima):
                                    steps.append(("split", g + 1))
                            if at == int(0.86 * n):
                                steps.append(("turn", g + 1))
                    if q > 0:
                        steps.append(("values", g, pcs[q - 1]))
                steps.append(("values", g, pcs[-1]))
            steps += [("evac", G - 1), ("out", G - 1)]
            return steps

        def attend(causal):
            steps = order(causal)
            rings = [s for s in steps if s[0] in ("max", "turn", "out")]
            scores = [s for s in steps if s[0] == "score"]
            values = [s for s in steps if s[0] == "values"]
            ring_at = {s: i for i, s in enumerate(rings)}
            score_at = {s: i for i, s in enumerate(scores)}
            value_at = {s: i for i, s in enumerate(values)}
            last_max = {g: max(i for i, s in enumerate(rings) if s[:2] == ("max", g)) for g in range(G)}
            pcs = pieces(causal)

            def diagonal(piece):
                return causal and piece[2] == piece[0] * P

            diag_at, count = {}, 0
            for s in scores:
                count += diagonal(s[3])
                diag_at[s] = count

            def ring(i):
                return PS[:, (4 + 2 * (i % 2)) * BANK:(6 + 2 * (i % 2)) * BANK]

            with nc.Block() as block:
                @block.tensor
                def _(pe):
                    def ring_slot(s):
                        i = ring_at[s]
                        if i >= 2:
                            pe.wait_ge(as_["ring_free"], i - 1)
                        return ring(i)

                    for s in steps:
                        if s[0] == "max":
                            _, g, j, qt = s
                            slot, h = ring_slot(s), 4 * g + j
                            width = (qt + 1) * P if causal else S
                            for c in range(0, width, BANK):
                                w = min(BANK, width - c)
                                tail = causal and c + w == width
                                last = pe.matmul(slot[:, c:c + w], QS[:, h // 2, qt * P:(qt + 1) * P], KZ[:, h, c:c + w],
                                                 start=True, stop=not tail)
                            if causal:
                                last = pe.matmul(slot[:, width - P:width], identb[:, :], negmask[:, :],
                                                 start=False, stop=True)
                            last.then_inc(as_["ring_full"], 1)
                        elif s[0] == "turn":
                            g = s[1]
                            slot = ring_slot(s).bitcast(BF16)
                            pe.wait_ge(as_["split_done"], g + 1)
                            for qt in range(T):
                                last = pe.transpose(slot[0:4 * NC_ROWS, qt * P:(qt + 1) * P],
                                                    CT[:, g % 2, qt, :, :].rearrange("p a b -> p (a b)"), identb[:, :])
                            last.then_inc(as_["ring_full"], 1)
                        elif s[0] == "score":
                            _, g, j, (kt, half, lo, hi) = s
                            n, h = score_at[s], 4 * g + j
                            if s[3] == pcs[0] and j == 0:
                                pe.wait_ge(as_["max_loaded"], 64 * (g + 1))
                            if n >= 2:
                                pe.wait_ge(as_["exp_done"], n - 1)
                            pe.matmul(bank(2 + n % 2, hi - lo), KZ[:, h, kt * P:(kt + 1) * P], QS[:, h // 2, lo:hi],
                                      start=True, stop=True).then_inc(as_["scores"], 1)
                        elif s[0] == "values":
                            _, g, piece = s
                            kt, half, lo, hi = piece
                            final = max(p[0] for p in pcs if p[1] == half)
                            newest = ("score", g, 3, piece)
                            pe.wait_ge(as_["exp_done"], score_at[newest] + 1)
                            if diagonal(piece):
                                pe.wait_ge(as_["diag_done"], diag_at[newest])
                            if kt == 0 and g > 0:
                                pe.wait_ge(as_["o_evac"], 2 * (g - 1) + half + 1)
                            for j in range(4):
                                last = pe.matmul(PS[32 * j:32 * j + 32, lo:hi], V[:, kt, 4 * g + j, :],
                                                 EXPS[:, kt % 2, j, lo:hi], start=(kt == 0), stop=(kt == final))
                            last.then_inc(as_["pv_done"], 1)
                        elif s[0] == "out":
                            g = s[1]
                            slot = ring_slot(s)
                            pe.wait_ge(as_["o_evac"], 2 * (g + 1))
                            for t in range(T):
                                last = pe.transpose(slot[:, t * P:(t + 1) * P], OT[:, t * P:(t + 1) * P], ident[:, :])
                            last.then_inc(as_["ring_full"], 1)

                @block.scalar
                def _(act):
                    act.activation(EPS[:, 3:4], EPS[:, 2:3], ACT.Exp)
                    for s in steps:
                        if s[0] == "score":
                            _, g, j, (kt, half, lo, hi) = s
                            n = score_at[s]
                            former = [v for v in values[:value_at[("values", g, s[3])]] if v[2][0] % 2 == kt % 2
                                      and (v[1], v[2][0]) != (g, kt)]
                            if former:
                                act.wait_ge(as_["pv_done"], value_at[former[-1]] + 1)
                            act.wait_ge(as_["scores"], n + 1)
                            act.activation(EXPS[:, kt % 2, j, lo:hi], bank(2 + n % 2, hi - lo), ACT.Exp)\
                               .then_inc(as_["exp_done"], 1)
                        elif s[0] == "evac":
                            g = s[1]
                            act.wait_ge(as_["pv_done"], value_at[("values", g, pcs[-1])] + 1)
                            if g > 0:
                                act.wait_ge(as_["ring_full"], ring_at[("out", g - 1)] + 1)
                            for half in range(HALVES):
                                act.activation(OT[:, half * BANK:(half + 1) * BANK], bank(half), ACT.Copy)\
                                   .then_inc(as_["o_evac"], 1)

                @block.vector
                def _(dve):
                    chain = [0]

                    def link(ins):
                        chain[0] += 1
                        ins.then_inc(as_["a_chain"], 1)
                        dve.wait_ge(as_["a_chain"], chain[0])

                    for s in rings:
                        i = ring_at[s]
                        if s[0] == "max":
                            _, g, j, qt = s
                            width = (qt + 1) * P if causal else S
                            if g >= 2:
                                dve.wait_ge(as_["split_done"], g - 1)
                            dve.wait_ge(as_["ring_full"], i + 1)
                            dve.tensor_reduce(NM[:, g % 2, qt, j:j + 1], ring(i)[:, 0:width], AXX, ALU.max,
                                              negate=True).then_inc(as_["ring_free"], 1)
                        elif s[0] == "turn":
                            g = s[1]
                            if g >= 2:
                                dve.wait_ge(as_["max_loaded"], 64 * (g - 1))
                            dve.wait_ge(as_["ring_full"], i + 1)
                            dve.tensor_copy(CTS[:, g % 2, :], ring(i).bitcast(BF16)[0:4 * NC_ROWS, 0:S])\
                               .then_inc(as_["ring_free"], 1)
                        else:
                            g = s[1]
                            dve.wait_ge(as_["ring_full"], i + 1)
                            o = ring(i).rearrange("p (t j c) -> p t j c", t=T, j=4)
                            if g > 0:
                                dve.wait_ge(as_["ring_free"], ring_at[("out", g - 1)] + 1)
                            link(dve.reciprocal(RD[:, :, :], o[:, :, :, HD]))
                            dve.tensor_tensor(AO[:, :, 32 * g:32 * (g + 1)].rearrange("p t (j d) -> p t j d", j=4),
                                              o[:, :, :, 0:HD], RD[:, :, :].unsqueeze(3).to_broadcast([P, T, 4, HD]),
                                              ALU.mult).then_inc(as_["ring_free"], 1)

                @block.gpsimd
                def _(pool):
                    chain = [0]

                    def link(ins):
                        chain[0] += 1
                        ins.then_inc(as_["g_chain"], 1)
                        pool.wait_ge(as_["g_chain"], chain[0])

                    for s in steps:
                        if s[0] == "score" and diagonal(s[3]):
                            _, g, j, (kt, half, lo, hi) = s
                            pool.wait_ge(as_["exp_done"], score_at[s] + 1)
                            tile = EXPS[:, kt % 2, j, lo:lo + P]
                            pool.affine_select(out=tile, in_=tile, compare_op=ALU.is_ge, fill=0.0, base=0,
                                               pattern=[[1, P]], channel_multiplier=-1).then_inc(as_["diag_done"], 1)
                        elif s[0] == "split":
                            g = s[1]
                            pool.wait_ge(as_["ring_free"], last_max[g] + 1)
                            if g >= 2:
                                pool.wait_ge(as_["ring_full"], ring_at[("turn", g - 2)] + 1)
                            link(pool.tensor_copy(CT[:, g % 2, :, 0, :], NM[:, g % 2, :, :]))
                            link(pool.tensor_tensor(NR[:, :, :], NM[:, g % 2, :, :], CT[:, g % 2, :, 0, :], ALU.subtract))
                            link(pool.tensor_copy(CT[:, g % 2, :, 1, :], NR[:, :, :]))
                            pool.tensor_tensor(CT[:, g % 2, :, 2, :], NR[:, :, :], CT[:, g % 2, :, 1, :], ALU.subtract)\
                                .then_inc(as_["split_done"], 1)

                @block.sync
                def _(sp):
                    for g in range(G):
                        sp.wait_ge(as_["ring_free"], ring_at[("turn", g)] + 1)
                        for j in range(4):
                            row = HROWS * (j % 2) + EXTRA
                            sp.dma_start(QS[row:row + NC_ROWS, 2 * g + j // 2, :], CTS[j:4 * NC_ROWS:4, g % 2, :])\
                              .then_inc(as_["max_loaded"], 16)

            clear(as_)

        OSEMS = ("o_turned", "o_copied", "o_proj", "o_added")
        os_ = {n: sem(n) for n in OSEMS}

        def project(b):
            with nc.Block() as block:
                @block.tensor
                def _(pe):
                    for t in range(T):
                        last = pe.transpose(bank(t // 4)[:, (t % 4) * D:(t % 4 + 1) * D], AO[:, t, :], ident[:, :])
                        if t % 4 == 3:
                            last.then_inc(os_["o_turned"], 1)
                    for t in range(T):
                        pe.wait_ge(os_["o_copied"], t // 4 + 1)
                        last = pe.matmul(bank(2 + t // 4)[:, (t % 4) * D:(t % 4 + 1) * D], hT[:, t * P:(t + 1) * P],
                                         wcol("ao", 0, D), start=True, stop=True)
                        if t % 4 == 3:
                            last.then_inc(os_["o_proj"], 1)

                @block.scalar
                def _(act):
                    for half in range(HALVES):
                        act.wait_ge(os_["o_turned"], half + 1)
                        act.activation(hT[:, half * BANK:(half + 1) * BANK], bank(half), ACT.Copy)\
                           .then_inc(os_["o_copied"], 1)

                @block.vector
                def _(dve):
                    for half in range(HALVES):
                        dve.wait_ge(os_["o_proj"], half + 1)
                        rows = X[:, bass.ts(b * HALVES + half, BANK)]
                        dve.tensor_tensor(rows, rows, bank(2 + half), ALU.add)

            clear(os_)

        MSEMS = ("m_chain", "ao_turned", "ao_copied", "ao_proj", "y_ready", "y_squares", "y_sums", "y_root", "yn_ready",
                 "y_turned", "y_copied", "gate_ready", "gate_read", "logits", "router_exp", "ups", "acts", "tanhs",
                 "gated", "downs", "combined", "x_new", "stored")
        ms = {n: sem(n) for n in MSEMS}
        UPS = [("e0u", 0), ("e0u", 1), ("e3a", 0), ("e2a", 0), ("e2a", 1), ("e1g", 0), ("e1u", 0), ("e1g", 1), ("e1u", 1),
               ("e3b", 0), ("e3b", 1), ("e2b", 0), ("e2b", 1), ("e2c", 0), ("e2c", 1)]
        READS = {"e3b": [B1], "e2b": [A1[:, 0, :], A1[:, 1, :]], "e2c": [A2[:, 0, :], A2[:, 1, :]]}
        WRITES = {"e0u": H0, "e2a": A1, "e2b": A2, "e2c": A3, "e3b": B2}
        GELUS = [u for u in UPS if u[0] not in ("e1g", "e1u")]
        GATED = [u for u in UPS if u[0] in ("e1g", "e1u")]
        NUPS, NGELU, NGATED, UPRING = len(UPS), len(GELUS), len(GATED), 4
        HIDDEN = [H0, H1, A3, B2]

        def experts(b, store):
            def up_bank(i):
                return bank(2 + i % UPRING)

            with nc.Block() as block:
                @block.tensor
                def _(pe):
                    for c in range(HALVES):
                        if c:
                            pe.wait_ge(ms["y_copied"], c)
                        for t in range(4):
                            last = pe.transpose(bank(0)[:, t * P:(t + 1) * P], AO[:, 4 * c + t, :], ident[:, :])
                        last.then_inc(ms["ao_turned"], 1)
                        pe.wait_ge(ms["ao_copied"], c + 1)
                        if c:
                            pe.wait_ge(ms["gate_read"], c)
                        for t in range(4):
                            last = pe.matmul(bank(1)[:, t * OUTW:(t + 1) * OUTW], OT[:, t * P:(t + 1) * P],
                                             wcol("wo", KEEP0, D), start=True, stop=True)
                        last.then_inc(ms["ao_proj"], 1)
                        pe.wait_ge(ms["yn_ready"], c + 1)
                        for t in range(4):
                            last = pe.transpose(bank(0)[:, t * P:(t + 1) * P], SQ[:, 1, t * P:(t + 1) * P], ident[:, :])
                        last.then_inc(ms["y_turned"], 1)
                        pe.wait_ge(ms["y_copied"], c + 1)
                        for t in range(4):
                            last = pe.matmul(bank(1)[:, 4 * OUTW + t * E:4 * OUTW + (t + 1) * E], YT[:, t * P:(t + 1) * P],
                                             wcol("gate", 0, E), start=True, stop=True)
                        last.then_inc(ms["gate_ready"], 1)
                        for n, (name, chunk) in enumerate(UPS):
                            i = c * NUPS + n
                            if i >= UPRING:
                                fc, old = divmod(i - UPRING, NUPS)
                                if UPS[old] in GATED:
                                    pe.wait_ge(ms["gated"], fc * NGATED + GATED.index(UPS[old]) + 1)
                                else:
                                    pe.wait_ge(ms["acts"], fc * NGELU + GELUS.index(UPS[old]) + 1)
                            src = READS.get(name, [YT])
                            if name in READS:
                                need = {"e3b": ("e3a", 0), "e2b": ("e2a", 1), "e2c": ("e2b", 1)}[name]
                                pe.wait_ge(ms["acts"], c * NGELU + GELUS.index(need) + 1)
                            for k, rows in enumerate(src):
                                at = k * FFN_HID + chunk * P
                                last = pe.matmul(up_bank(i), wcol(name, at, at + P), rows,
                                                 start=(k == 0), stop=(k == len(src) - 1))
                            last.then_inc(ms["ups"], 1)
                        pe.wait_ge(ms["gated"], (c + 1) * NGATED)
                        pe.wait_ge(ms["acts"], (c + 1) * NGELU)
                        for t in range(4):
                            i = 4 * c + t
                            if i >= 2:
                                pe.wait_ge(ms["combined"], i - 1)
                            for e in range(E):
                                for k in range(2):
                                    last = pe.matmul(bank(6 + i % 2)[:, e * OUTW:(e + 1) * OUTW],
                                                     HIDDEN[e][:, k, t * P:(t + 1) * P],
                                                     wcol(f"d{e}", k * D + KEEP0, (k + 1) * D), start=(k == 0), stop=(k == 1))
                            last.then_inc(ms["downs"], 1)

                @block.scalar
                def _(act):
                    for c in range(HALVES):
                        act.wait_ge(ms["ao_turned"], c + 1)
                        act.activation(OT[:, 0:BANK], bank(0), ACT.Copy).then_inc(ms["ao_copied"], 1)
                        act.wait_ge(ms["y_ready"], c + 1)
                        act.activation(SQ[:, 0, 0:BANK], U[:, 4 * c:4 * c + 4, :].rearrange("p t d -> p (t d)"),
                                       ACT.Square).then_inc(ms["y_squares"], 1)
                        act.wait_ge(ms["y_sums"], c + 1)
                        act.activation(R2[:, :], R2[:, :], ACT.Sqrt, bias=EPS[:, 1:2], scale=1.0 / D)\
                           .then_inc(ms["y_root"], 1)
                        act.wait_ge(ms["y_turned"], c + 1)
                        if c:
                            act.wait_ge(ms["ups"], c * NUPS)
                        act.activation(YT[:, :], bank(0), ACT.Copy).then_inc(ms["y_copied"], 1)
                        act.wait_ge(ms["logits"], c + 1)
                        act.activation(RT[:, 4, :, :], RT[:, 3, :, :], ACT.Exp).then_inc(ms["router_exp"], 1)
                        for n, (name, chunk) in enumerate(UPS):
                            i = c * NUPS + n
                            if name == "e1u":
                                continue
                            act.wait_ge(ms["ups"], i + 1)
                            if c and n == 0:
                                act.wait_ge(ms["downs"], 4 * c)
                            if name == "e1g":
                                if chunk == 0 and c:
                                    act.wait_ge(ms["gated"], c * NGATED)
                                act.activation(TH[:, chunk, :], up_bank(i), ACT.Tanh, scale=0.5).then_inc(ms["tanhs"], 1)
                            else:
                                to = B1 if name == "e3a" else WRITES[name][:, chunk, :]
                                act.activation(to, up_bank(i), ACT.Gelu).then_inc(ms["acts"], 1)

                @block.vector
                def _(dve):
                    chain = [0]

                    def link(ins):
                        chain[0] += 1
                        ins.then_inc(ms["m_chain"], 1)
                        dve.wait_ge(ms["m_chain"], chain[0])

                    def wide(small):
                        return small.unsqueeze(2).to_broadcast([P, 4, E])

                    for c in range(HALVES):
                        tiles = slice(4 * c, 4 * c + 4)
                        kept = U[:, tiles, KEEP0:D]
                        dve.wait_ge(ms["ao_proj"], c + 1)
                        dve.tensor_tensor(kept, kept, bank(1)[:, 0:4 * OUTW].rearrange("p (t n) -> p t n", t=4),
                                          ALU.add).then_inc(ms["y_ready"], 1)
                        dve.wait_ge(ms["y_squares"], c + 1)
                        dve.tensor_reduce(R2[:, :], SQ[:, 0, 0:BANK].rearrange("p (t d) -> p t d", t=4), AXX, ALU.add)\
                           .then_inc(ms["y_sums"], 1)
                        dve.wait_ge(ms["y_root"], c + 1)
                        link(dve.reciprocal(R2[:, :], R2[:, :]))
                        dve.tensor_tensor(SQ[:, 1, 0:BANK].rearrange("p (t d) -> p t d", t=4), U[:, tiles, :],
                                          R2[:, :].unsqueeze(2).to_broadcast([P, 4, D]), ALU.mult)\
                           .then_inc(ms["yn_ready"], 1)
                        dve.wait_ge(ms["gate_ready"], c + 1)
                        dve.memset(RT[:, 1, :, :], 0.0)
                        dve.tensor_copy(RT[:, 0, :, :], bank(1)[:, 4 * OUTW:4 * OUTW + 4 * E]
                                        .rearrange("p (t e) -> p t e", t=4)).then_inc(ms["gate_read"], 1)
                        dve.wait_ge(ms["gate_read"], c + 1)
                        link(dve.tensor_tensor(RT[:, 2, :, :].bitcast(I32), RT[:, 0, :, :], RT[:, 0, :, :], ALU.is_equal))
                        link(dve.copy_predicated(RT[:, 1, :, :], RT[:, 2, :, :].bitcast(I32), RT[:, 0, :, :]))
                        link(dve.tensor_scalar(RT[:, 1, :, :], RT[:, 1, :, :], FMAX, -FMAX, ALU.min, ALU.max))
                        link(dve.tensor_reduce(RS[:, 0, :], RT[:, 1, :, :], AXX, ALU.max))
                        dve.tensor_tensor(RT[:, 3, :, :], RT[:, 1, :, :], wide(RS[:, 0, :]), ALU.subtract)\
                           .then_inc(ms["logits"], 1)
                        dve.wait_ge(ms["router_exp"], c + 1)
                        link(dve.tensor_reduce(RS[:, 1, :], RT[:, 4, :, :], AXX, ALU.add))
                        link(dve.reciprocal(RS[:, 1, :], RS[:, 1, :]))
                        link(dve.tensor_tensor(RT[:, 5, :, :], RT[:, 4, :, :], wide(RS[:, 1, :]), ALU.mult))
                        for j in range(E):
                            for lo, hi, op in ((0, j, ALU.is_gt), (j + 1, E, ALU.is_ge)):
                                if lo < hi:
                                    last = dve.tensor_tensor(CMP[:, :, lo:hi, j],
                                                             RT[:, 5, :, j:j + 1].to_broadcast([P, 4, hi - lo]),
                                                             RT[:, 5, :, lo:hi], op)
                        link(last)
                        link(dve.tensor_reduce(RT[:, 6, :, :], CMP[:, :, :, :], AXX, ALU.add))
                        link(dve.tensor_scalar(RT[:, 7, :, :], RT[:, 6, :, :], 2.0, None, ALU.is_lt))
                        link(dve.tensor_tensor(RT[:, 8, :, :], RT[:, 7, :, :], RT[:, 5, :, :], ALU.mult))
                        link(dve.tensor_reduce(RS[:, 2, :], RT[:, 8, :, :], AXX, ALU.add))
                        link(dve.tensor_scalar(RS[:, 2, :], RS[:, 2, :], 1e-8, None, ALU.add))
                        link(dve.reciprocal(RS[:, 2, :], RS[:, 2, :]))
                        link(dve.tensor_tensor(RT[:, 9, :, :], RT[:, 8, :, :], wide(RS[:, 2, :]), ALU.mult))
                        for n, (name, chunk) in enumerate(UPS):
                            i = c * NUPS + n
                            if name == "e1g":
                                dve.wait_ge(ms["tanhs"], 2 * c + chunk + 1)
                                dve.scalar_tensor_tensor(TH[:, chunk, :], TH[:, chunk, :], 1.0, up_bank(i),
                                                         ALU.add, ALU.mult).then_inc(ms["gated"], 1)
                            elif name == "e1u":
                                dve.wait_ge(ms["ups"], i + 1)
                                dve.wait_ge(ms["gated"], c * NGATED + GATED.index((name, chunk)))
                                if c and chunk == 0:
                                    dve.wait_ge(ms["downs"], 4 * c)
                                dve.scalar_tensor_tensor(H1[:, chunk, :], TH[:, chunk, :], 0.5, up_bank(i),
                                                         ALU.mult, ALU.mult).then_inc(ms["gated"], 1)
                        for t in range(4):
                            i = 4 * c + t
                            dve.wait_ge(ms["downs"], i + 1)
                            dve.tensor_tensor(WD[:, i % 2, :, :],
                                              bank(6 + i % 2)[:, 0:E * OUTW].rearrange("p (e n) -> p e n", e=E),
                                              RT[:, 9, t, :].unsqueeze(2).to_broadcast([P, E, OUTW]), ALU.mult)\
                                .then_inc(ms["combined"], 1)
                            dve.wait_ge(ms["combined"], i + 1)
                            link(dve.tensor_reduce(WS[:, i % 2, :], WD[:, i % 2, :, :].rearrange("p e n -> p n e"),
                                                   AXX, ALU.add))
                            last = dve.tensor_tensor(U[:, i, KEEP0:D], U[:, i, KEEP0:D], WS[:, i % 2, :], ALU.add)
                        link(last)
                        rows = X[:, bass.ts(b * HALVES + c, BANK)]
                        dve.scalar_tensor_tensor(rows, U[:, tiles, :].rearrange("p t d -> p (t d)"), 0.5, rows,
                                                 ALU.mult, ALU.add).then_inc(ms["x_new"], 1)

                if store:
                    @block.sync
                    def _(sp):
                        to = out.rearrange("b (t p) d -> p (b t) d", p=P)
                        for c in range(HALVES):
                            sp.wait_ge(ms["x_new"], c + 1)
                            sp.dma_start(to[:, bass.ts(b * HALVES + c, 4), :],
                                         X[:, bass.ts(b * HALVES + c, BANK)].rearrange("p (t d) -> p t d", t=4))\
                              .then_inc(ms["stored"], 16)
                        sp.wait_ge(ms["stored"], 16 * HALVES)

            clear(ms)

        def sublayer(ffn, store=False):
            with nc.Fori(0, B) as b:
                prep(b, ffn)
                attend(causal=ffn)
                if ffn:
                    experts(b, store)
                else:
                    project(b)

        sublayer(ffn=True)
        sublayer(ffn=False)
        sublayer(ffn=True, store=True)


def kernel(**inputs):
    import numpy as _np
    import concourse.bacc as _bacc
    from concourse import mybir as _mybir
    from concourse.bass_utils import run_bass_kernel_spmd as _run

    a = {k: _np.asarray(v) for k, v in inputs.items()}

    def up(name):
        return a["L0_ffn_" + name].T

    def two(w):
        return _np.concatenate([w[:P], w[P:]], axis=1)

    def per_head(w):
        return _np.repeat(w.reshape(D, KV, HD), H // KV, axis=1).reshape(D, H * HD)

    at = {"wq": up("wq"), "wk": up("wk"), "wv": up("wv"), "gate": up("gate_w"), "e0u": up("e0_up"),
          "e1g": up("e1_w1"), "e1u": up("e1_w2"), "e2a": up("e2_l1"), "e3a": up("e3_down"), "wo": up("wo"),
          "e2b": two(up("e2_l2")), "e2c": two(up("e2_l3")), "e3b": up("e3_up"),
          "d0": two(up("e0_down")), "d1": two(up("e1_down")), "d2": two(up("e2_l4")), "d3": two(up("e3_out")),
          "aq": a["L0_attn_Wq"], "ak": per_head(a["L0_attn_Wk"]), "av": per_head(a["L0_attn_Wv"]), "ao": a["L0_attn_Wo"]}
    weights = _np.ascontiguousarray(_np.concatenate([at[name] for name, _ in WPARTS], axis=1))
    vectors = _np.ascontiguousarray(_np.stack([a["L0_ffn_n1_w"], a["L0_ffn_n2_w"], _np.tile(a["L0_ffn_qn_w"], H),
                                               _np.tile(a["L0_ffn_kn_w"], H)], axis=1))
    key, query = additive_rows()
    bf16 = _mybir.dt.np(_mybir.dt.bfloat16)
    key = _np.ascontiguousarray(_np.repeat(key[:, None, :], H // 2, axis=1)).astype(bf16)
    arrays = {"x": _np.ascontiguousarray(a["L0_attn_x"]), "weights": weights, "vectors": vectors,
              "key_rows": key, "query_rows": query.astype(bf16)}

    nc = _bacc.Bacc("TRN2", target_bir_lowering=False, num_devices=1)
    args = [nc.dram_tensor(name, v.shape, _mybir.dt.from_np(v.dtype), kind="ExternalInput").ap()
            for name, v in arrays.items()]
    out = nc.dram_tensor("out", (B, S, D), FP32, kind="ExternalOutput").ap()
    macaron_kernel(nc, *args, out)
    r = _run(nc, [arrays], core_ids=[0])
    return r.results[0]["out"]
```

```python
import math
from contextlib import ExitStack

import numpy as np
import concourse.bass as bass
from concourse import mybir

FP32 = mybir.dt.float32
BF16 = mybir.dt.bfloat16
I32 = mybir.dt.int32
ALU = mybir.AluOpType
ACT = mybir.ActivationFunctionType
AXX = mybir.AxisListType.X

B, S, D = 4, 1024, 128
P = 128
T = S // P
H, HD = 16, 8
KV = 4
G = H // 4
BANK = 512
HALVES = S // BANK
FFN_HID = 256
KEEP0 = 32
OUTW = D - KEEP0
E = 4
LN_EPS = 1e-5
RMS_EPS = 1.1920929e-07
SCALE = float(np.float32(HD ** -0.5))
FMAX = float(np.finfo(np.float32).max)
MASKED = -1.0e30

QPART = (0, 0, 0, 1, 1, 2)
KPART = (0, 1, 2, 0, 1, 0)
HROWS = 64
EXTRA = HD * len(QPART)
NC_ROWS = 3
NEXTRA = HROWS - EXTRA


def f32_parts(v):
    out, rest = [], np.float32(v)
    for _ in range(3):
        bits = np.array(rest, np.float32).view(np.uint32).astype(np.uint64)
        r = ((bits + 0x7FFF + ((bits >> 16) & 1)) >> 16 << 16).astype(np.uint32).view(np.float32)
        out.append(np.float32(r))
        rest = np.float32(rest - np.float32(r))
    return out


def additive_rows():
    key = np.zeros((NEXTRA, S), np.float32)
    key[0:NC_ROWS] = 1.0
    rel = np.arange(S) - (S - 1)
    low = rel % 4
    for n in range(3):
        key[NC_ROWS + 2 * n] = rel - low
        key[NC_ROWS + 2 * n + 1] = low
    query = np.zeros((2, NEXTRA, H, S), np.float32)
    start = 2.0 ** (-2.0 ** (-(math.log2(H) - 3)))
    for h in range(H):
        for n, part in enumerate(f32_parts(np.float32(start * start ** h))):
            query[1, NC_ROWS + 2 * n, h] = part
            query[1, NC_ROWS + 2 * n + 1, h] = part
    return key, query


ROWS = [(4 * g + 2 * q + e, d) for g in range(4) for e in range(2) for d in range(HD) for q in range(2)]
ROW_FEATURE = np.array([h * HD + d for h, d in ROWS])
ROW_HEAD = np.array([h for h, _ in ROWS])
ROWS_HEADS = np.array([4 * g + 2 * q + e for g in range(4) for e in range(2) for q in range(2)])


def columns(parts):
    at, out = 0, {}
    for name, width in parts:
        out[name] = at
        at += width
    return out, at


WPARTS = [("wq", D), ("wk", D), ("wv", D),
          ("gate", E), ("e0u", 256), ("e1g", 256), ("e1u", 256), ("e2a", 256), ("e3a", 128),
          ("wo", D), ("e2b", 512), ("e2c", 512), ("e3b", 256),
          ("d0", 256), ("d1", 256), ("d2", 256), ("d3", 256),
          ("aq", D), ("ak", D), ("av", D), ("ao", D)]
WAT, WCOLS = columns(WPARTS)






def pieces(causal):
    out = []
    for kt in range(T):
        for half in range(HALVES):
            lo = max(half * BANK, kt * P if causal else 0)
            if lo < (half + 1) * BANK:
                out.append((kt, half, lo, (half + 1) * BANK))
    return out


def max_steps(g, causal):
    out = []
    for j in range(4):
        for qt in (7, 0, 6, 1, 5, 2, 4, 3):
            width = (qt + 1) * P if causal else S
            for lo in range(0, width, BANK):
                out.append(("max", g, j, qt, lo, min(lo + BANK, width)))
    return out


def prep_steps(ffn):
    out = [("p_stats",)]
    for h in range(HALVES):
        out += [("p_norm", h), ("p_turn", h), ("p_qk", h, 0), ("p_qk", h, 1), ("p_v", h)]
        if ffn:
            out += [("p_square", h, 0), ("p_square", h, 1), ("p_sum", h), ("p_root", h), ("p_spread", h, 0),
                    ("p_spread", h, 1)]
        out += [("p_split", h, w, n) for n in range(4) for w in range(2)] + [("p_store", h, 0), ("p_store", h, 1)]
    return out


UPS1 = [("e0u", 0), ("e0u", 1), ("e2a", 0), ("e2a", 1), ("e3a", 0)]
UPSG = [("e1g", 0), ("e1u", 0), ("e1g", 1), ("e1u", 1)]
UPS2 = [("e3b", 0), ("e3b", 1), ("e2b", 0), ("e2b", 1)]
UPS3 = [("e2c", 0), ("e2c", 1)]


def expert_steps(ffn):
    out = [("m_aturn", h) for h in range(HALVES)]
    if not ffn:
        return out + [("m_out", h) for h in range(HALVES)]
    for c in range(HALVES):
        out += [("m_u", c), ("m_ao", c), ("m_square", c), ("m_rms", c), ("m_norm", c), ("m_yturn", c), ("m_gate", c)]
        out += [("m_up", c) + u for u in UPS1]
        out += [("m_logits", c), ("m_rexp", c), ("m_gelu", c, 0), ("m_route", c)]
        out += [("m_up", c) + u for u in UPSG + UPS2] + [("m_gelu", c, 1)]
        out += [("m_up", c) + u for u in UPS3] + [("m_gelu", c, 2)]
        out += [("m_down", c, t) for t in range(4)] + [("m_x", c)]
    return out


def step_cost(s, causal):
    kind = s[0]
    fp32 = 0.86
    if kind == "max":
        n = s[5] - s[4]
        return [("pe", 0.015 + n / 2400 + (0.07 if causal and s[5] == (s[3] + 1) * P else 0)), ("dve", 0.07 + n / 960)]
    if kind == "score":
        lo, hi = s[3][2:]
        diagonal = causal and lo == s[3][0] * P
        return [("pe", 0.015 + (hi - lo) / 2400), ("act", 0.05 + (hi - lo) / 1180)] + [("pool", 0.4)] * bool(diagonal)
    if kind == "values":
        return [("pe", 0.04 + 0.92 * (s[2][3] - s[2][2]) / BANK)]
    return {
        "split": [("dve", 0.2), ("pool", 2.2)], "turn": [("pe", 0.5), ("dve", 1.2), ("sp", 2.2), ("wire", 2.0)],
        "evac": [("act", 1.05)], "out": [("pe", 0.43), ("dve", 0.6)],
        "stack": [("sp", 10.5), ("wire", 2.0)], "v_copy": [("pool", 2.0)],
        "p_stats": [("dve", 3.0), ("pool", 5.0)], "p_norm": [("dve", 0.8)], "p_turn": [("pe", 0.43), ("act", 0.5)],
        "p_qk": [("pe", fp32), ("act", 0.5)], "p_v": [("pe", fp32), ("act", 0.5)], "p_square": [("pool", 1.3)],
        "p_sum": [("pe", 1.0), ("dve", 1.1)], "p_root": [("act", 3.5)],
        "p_spread": [("pe", 0.43), ("dve", 0.7)],
        "p_split": [("pool", 1.3) if s[-1] in (1, 3) else ("act", 0.5)], "p_store": [("sp", 0.6), ("wire", 2.0)],
        "m_aturn": [("pe", 0.43), ("act", 0.5)], "m_out": [("pe", fp32), ("dve", 0.7)], "m_u": [("dve", 0.8)],
        "m_ao": [("pe", 0.75), ("dve", 0.6)], "m_square": [("pool", 1.3)], "m_rms": [("dve", 0.6)],
        "m_norm": [("pool", 2.3)], "m_yturn": [("pe", 0.43), ("act", 0.5)], "m_gate": [("pe", 0.45), ("dve", 0.15)],
        "m_logits": [("dve", 0.9)], "m_rexp": [("act", 0.2)], "m_route": [("dve", 2.5)],
        "m_up": [("pe", fp32 * (2 if s[2:3] in (("e2b",), ("e2c",)) else 1))] + [("act", 0.5)] * (s[2:3] == ("e1g",))
                + [("dve", 0.7)],
        "m_gelu": [("act", (4.7, 4.3, 3.5)[s[-1]] if kind == "m_gelu" else 0)],
        "m_down": [("pe", 1.55), ("dve", 1.5)], "m_x": [("dve", 0.6), ("sp", 0.6)],
    }[kind]


RING_STEPS = ("max", "score", "turn", "out", "p_turn", "p_qk", "p_v", "p_sum", "p_spread", "m_aturn", "m_ao", "m_out",
              "m_yturn", "m_gate", "m_up", "m_down")
PIECES = 4
RING = 6


def search_order(attn, prepared, finished, idle_act, idle_dve, late_price, slack, shift):
    pcs = pieces(attn) if attn is not None else []
    kind = {g: (attn if g < G else prepared) for g in range(G + 3)}
    streams = []

    def stream(name, steps, until):
        if steps:
            streams.append((name, steps, until))

    groups = range(G) if attn is not None else ()
    maxed = [g for g in range(1 if attn is not None else 4, 5) if kind[g] is not None]
    stream("scores", [("score", g, j, piece) for g in groups for piece in pcs for j in range(4)], 0.99)
    stream("values", [s for g in groups for s in [("values", g, piece) for piece in pcs] + [("evac", g)]], 1.0)
    stream("outs", [("out", g, h) for g in groups for h in range(HALVES)], 1.0)
    stream("maxima", [s for g in maxed for s in max_steps(g, kind[g]) + [("split", g), ("turn", g)]], 0.92)
    stream("experts", expert_steps(finished) if finished is not None else [], 0.93)
    stream("projections", prep_steps(prepared) if prepared is not None else [], 0.45)
    loads = ([3] if attn is not None else []) + ([4, 5, 6] if prepared is not None else [])
    stream("stacks", [("stack", g) for g in loads], 0.0)
    stream("v_copies", [("v_copy", g) for g in loads], 0.0)

    def needs(s):
        k, g = s[0], s[1] if len(s) > 1 else None
        if k == "max":
            return [("stack", g)] if g in loads else []
        if k == "score":
            _, g, j, (kt, half, lo, hi) = s
            out = [("turn", g)] if g > 0 else []
            n = pcs.index(s[3]) - PIECES
            return out + ([("values", g, pcs[n])] if n >= 0 else [("values", g - 1, pcs[n])] if g > 0 else [])
        if k == "values":
            out = [("score", g, 3, s[2])]
            if s[2][0] == 0 and g > 0:
                out += [("evac", g - 1)]
            return out + ([("v_copy", 3)] if g == G - 1 and s[2][0] == 0 else [])
        if k == "evac":
            return [("out", g - 1, 1)] if g > 0 else []
        if k == "out":
            return [("evac", g)] + ([("m_aturn", s[2])] if finished is not None else [])
        if k == "stack" and g >= G:
            return [("p_store", 1, 1)] + ([("score", g - G, 3, pcs[-1])] if attn is not None else [])
        if k == "v_copy" and g >= G:
            return [("p_v", 1)] + ([("values", g - G, pcs[-1])] if attn is not None else [])
        if k == "p_v":
            return [("v_copy", 3)] if attn is not None else []
        if k == "p_store":
            return [("stack", 3)] if attn is not None else []
        return []

    waits_for = {"m_ao": ("m_u", "m_aturn"), "m_rms": ("m_square",), "m_norm": ("m_rms",), "m_yturn": ("m_norm",),
                 "m_gate": ("m_yturn",), "m_square": ("m_ao",), "m_logits": ("m_gate",), "m_rexp": ("m_logits",),
                 "m_route": ("m_rexp",), "m_out": ("m_aturn",), "p_norm": ("p_stats",), "p_turn": ("p_norm",),
                 "p_qk": ("p_turn",), "p_v": ("p_turn",), "p_square": ("p_qk",), "p_sum": ("p_square",),
                 "p_root": ("p_sum",), "p_spread": ("p_root",), "p_split": ("p_spread", "p_qk", "p_split"),
                 "p_store": ("p_split",),
                 "split": ("max",), "turn": ("split",), "m_down": ("m_gelu",), "evac": ("values",)}

    def needs_own(s):
        if s[0] == "m_up":
            return ("m_gelu",) if s[2] in ("e3b", "e2b", "e2c") else ("m_yturn",)
        if s[0] == "m_gelu":
            return ("m_up",)
        return waits_for.get(s[0], ())

    steps = [s for _, part, _ in streams for s in part]
    number = {s: n for n, s in enumerate(steps)}
    first = [number[part[0]] for _, part, _ in streams]
    end = [number[part[-1]] + 1 for _, part, _ in streams]
    costs = [[(ENGINES.index(e), us) for e, us in step_cost(s, kind.get(s[1]) if s[0] in ("max", "score") else None)]
             for s in steps]
    work = [sum(us for c in costs for e, us in c if e == n) for n in range(len(ENGINES))]
    needed, due = [], []
    for name, part, until in streams:
        newest = {}
        for n, s in enumerate(part):
            needed.append([number[m] for m in needs(s)] + [newest[k] for k in needs_own(s) if k in newest])
            due.append(work[0] * until * n / len(part) + shift.get(name, 0.0))
            newest[s[0]] = number[s]
    loads_only = [ENGINES[c[0][0]] in ("sp", "pool") for c in costs]

    def extended(state):
        _, at, clock, busy, done, ring, plan = state
        found = []
        for k, n in enumerate(at):
            if n == end[k] or any(done[m] is None for m in needed[n]):
                continue
            ready = max([done[m] for m in needed[n]] + [0.0])
            after, used = list(clock), list(busy)
            early = loads_only[n] and max(ready, clock[costs[n][0][0]]) > clock[0] + 0.5
            if steps[n][0] in RING_STEPS and len(ring) == RING:
                ready = max(ready, ring[0])
            for e, us in costs[n]:
                start = max(ready, after[e])
                if ENGINES[e] != "wire":
                    after[e] = start + us
                used[e] += us
                ready = start + us + SIGNAL
            found.append((loads_only[n] and not early, early, k, n, after, used, ready))
        chosen = [f for f in found if f[0]][:1] or [f for f in found if not f[1]] or [min(found, key=lambda f: f[6])]
        out = []
        for _, _, k, n, after, used, ready in chosen:
            now = used[0]
            late = sum(max(0.0, now - due[m] - slack) for q, m in enumerate(at[:k] + (n + 1,) + at[k + 1:]) if m < end[q])
            price = (1 + 0.02) * (after[0] - now) + late_price * late
            for e, weight in ((1, idle_act), (2, idle_dve)):
                price += weight * (max(after[e], after[0]) - used[e] - (work[0] - work[e]) * now / work[0])
            out.append((price, at[:k] + (n + 1,) + at[k + 1:], after, used, done,
                        (ring + (ready,))[-RING:] if steps[n][0] in RING_STEPS else ring, (plan, n, ready)))
        return out

    states = [(0.0, tuple(first), [0.0] * len(ENGINES), [0.0] * len(ENGINES), [None] * len(steps), (), None)]
    for _ in steps:
        best = {}
        for state in states:
            for new in extended(state):
                if new[1] not in best or new[0] < best[new[1]][0]:
                    best[new[1]] = new
        states = []
        for price, at, clock, busy, done, ring, plan in sorted(best.values(), key=lambda p: p[0])[:PLANS]:
            done = list(done)
            done[plan[1]] = plan[2]
            states.append((price, at, clock, busy, done, ring, plan))
    state = min(states, key=lambda p: max(p[2][:3]))
    order, plan = [], state[6]
    while plan is not None:
        plan, n, _ = plan
        order.append(steps[n])
    return order[::-1], max(state[2][:3])


def slot_order(attn, prepared, finished):
    found = [search_order(attn, prepared, finished, *weights) for weights in SEARCHES]
    return min(found, key=lambda f: f[1])[0]


ENGINES = ("pe", "act", "dve", "pool", "sp", "wire")
SIGNAL = 0.2
PLANS = 64
SEARCHES = [(0.2, 0.5, 0.02, 15.0, {"maxima": -10.0, "values": 2.0, "projections": -5.0}),
            (0.2, 0.7, 0.003, 4.0, {"maxima": -20.0, "values": 0.0, "projections": -20.0}),
            (0.7, 1.0, 0.01, 2.0, {"maxima": 0.0, "values": 2.0, "projections": -5.0})]


def macaron_kernel(nc, x, weights, vectors, head_of, key_rows, query_rows, out):
    ctx = ExitStack()
    with ctx:
        def sb(name, shape, dt):
            return ctx.enter_context(nc.sbuf_tensor(name, shape, dt))

        def sem(name):
            return ctx.enter_context(nc.semaphore(name))

        X = sb("X", [P, B * T * D], FP32)
        W = sb("W", [P, WCOLS], FP32)
        VEC = sb("VEC", [P, 4], FP32)
        EPS = sb("EPS", [P, 5], FP32)
        ident = sb("ident", [P, P], FP32)
        identb = sb("identb", [P, P], BF16)
        negmask = sb("negmask", [P, P], BF16)
        headsum = sb("headsum", [P, H], FP32)
        QS = sb("QS", [P, H // 2, S], BF16)
        KZ = sb("KZ", [P, 2, H // 2, S], BF16)
        V = sb("V", [P, T, H, 32], FP32)
        EXPS = sb("EXPS", [P, PIECES, 4, BANK], FP32)
        NM = sb("NM", [P, 2, T, 4], FP32)
        NR = sb("NR", [P, T, 4], FP32)
        CT = sb("CT", [P, T, NC_ROWS, 4], BF16)
        CTS = sb("CTS", [NC_ROWS * 4, S], BF16)
        OT = sb("OT", [P, S], FP32)
        RD = sb("RD", [P, T, 4], FP32)
        AO = sb("AO", [P, T, D], FP32)
        BST = sb("BST", [P, T, 6], FP32)
        MV = sb("MV", [P, T, 2], FP32)
        RSTD = sb("RSTD", [P, T], FP32)
        RR = sb("RR", [P, T], FP32)
        MVA = sb("MVA", [P, B * T * 2], FP32)
        RSTDA = sb("RSTDA", [P, B * T], FP32)
        HN = sb("HN", [P, 4, D], FP32)
        hT = sb("hT", [P, BANK], FP32)
        QK = sb("QK", [P, 2, BANK], FP32)
        SQ = sb("SQ", [P, 2, BANK], FP32)
        ROOT = sb("ROOT", [P, 2, 4, H], FP32)
        PARTS = sb("PARTS", [P, 2, 3, BANK], BF16)
        VS = sb("VS", [P, T, D], FP32)
        SCR = nc.dram_tensor("scratch_parts", [2, 3, P, S], BF16).ap()
        HID = sb("HID", [P, 12, BANK], FP32)
        H0, A1, B1, B2, A2, H1, YT = (HID[:, 0:2], HID[:, 2:4], HID[:, 4:5], HID[:, 5:7], HID[:, 7:9], HID[:, 9:11],
                                      HID[:, 11, :])
        A3, TH = A1, B2
        LEVELS = [HID[:, 0:5], HID[:, 5:9], HID[:, 2:4]]
        AOT = sb("AOT", [P, S], FP32)
        UM = sb("UM", [P, 4, D], FP32)
        YN = sb("YN", [P, 4, D], FP32)
        R2 = sb("R2", [P, 4], FP32)
        RT = sb("RT", [P, 10, 4, E], FP32)
        RS = sb("RS", [P, 3, 4], FP32)
        CMP = sb("CMP", [P, 4, E, E], FP32)
        WD = sb("WD", [P, 2, E, OUTW], FP32)
        WS = sb("WS", [P, 2, OUTW], FP32)

        PS = ctx.enter_context(nc.psum_tensor("PS", [P, 8 * BANK], FP32))

        def bank(n, width=BANK):
            return PS[:, n * BANK:n * BANK + width]

        def wcol(name, a=0, b=None):
            return W[:, WAT[name] + a:WAT[name] + b]

        loaded, zeroed, drawn = sem("loaded"), sem("zeroed"), sem("drawn")

        def clear(sems):
            for s in sems.values():
                nc.sync.sem_clear(s)
            nc.all_engine_barrier()

        with nc.Block() as block:
            @block.sync
            def _(sp):
                sp.dma_start(X[:, :].rearrange("p (n d) -> p n d", d=D), x.rearrange("b (t p) d -> p (b t) d", p=P))\
                  .then_inc(loaded, 16)
                sp.dma_start(VEC[:, :], vectors).then_inc(loaded, 16)
                sp.dma_start(W[:, :], weights).then_inc(loaded, 16)
                sp.dma_start(headsum[:, :], head_of).then_inc(loaded, 16)
                sp.wait_ge(zeroed, 2)
                for e in range(2):
                    rows = slice(HROWS * e + EXTRA, HROWS * (e + 1))
                    sp.dma_start(KZ[rows, e, :, :], key_rows)\
                      .then_inc(loaded, 16)
                sp.wait_ge(loaded, 16 * 6)

            @block.vector
            def _(dve):
                dve.memset(V[:, :, :, :], 0.0).then_inc(zeroed, 1)
                dve.memset(KZ[:, :, :, :].bitcast(I32), 0).then_inc(zeroed, 1)
                dve.wait_ge(zeroed, 2)
                dve.memset(V[:, :, :, HD:HD + 1], 1.0)
                dve.memset(CMP[:, :, :, :], 0.0)
                for n, value in enumerate((LN_EPS, RMS_EPS, 0.0, 0.0, -0.5)):
                    dve.memset(EPS[:, n:n + 1], value)
                dve.wait_ge(loaded, 16 * 6)
                for lo, hi, n in ((WAT["wq"], WAT["gate"], 0), (WAT["gate"], WAT["wo"], 1)):
                    dve.tensor_scalar(W[:, lo:hi], W[:, lo:hi], VEC[:, n:n + 1], None, ALU.mult)
                dve.tensor_scalar(VEC[:, 2:3], VEC[:, 2:3], SCALE, None, ALU.mult)

            @block.gpsimd
            def _(pool):
                pool.memset(ident[:, :], 0.0).then_inc(drawn, 1)
                pool.memset(identb[:, :], 0.0).then_inc(drawn, 1)
                pool.memset(negmask[:, :], 0.0).then_inc(drawn, 1)
                pool.wait_ge(drawn, 3)
                for m in (ident, identb):
                    pool.affine_select(out=m[:, :], in_=m[:, :], compare_op=ALU.not_equal, fill=1.0, base=0,
                                       pattern=[[-1, P]], channel_multiplier=1).then_inc(drawn, 1)
                pool.affine_select(out=negmask[:, :], in_=negmask[:, :], compare_op=ALU.is_ge, fill=MASKED, base=0,
                                   pattern=[[-1, P]], channel_multiplier=1).then_inc(drawn, 1)

        SEMS = ("t_scores", "t_values", "t_ring", "t_work",
                "s_exp", "s_evac", "s_work", "s_tanh", "s_gelu", "s_rexp", "s_root", "s_split",
                "v_ring", "v_max", "v_work", "v_chain", "v_stats", "v_norm", "v_root", "v_sums", "v_logits", "v_x",
                "g_chain", "g_diag", "g_split", "g_rr", "g_square", "g_parts", "g_msquare", "g_norm", "g_vcopy",
                "d_max", "d_stack3", "d_stack4", "d_stack5", "d_stack6", "d_scratch0", "d_scratch1", "d_out")
        sm = {n: sem(n) for n in SEMS}
        STACKED = 16 * 2 * (1 + 3 + 3)

        def slot(attn, b_attn, prepared=None, b_prep=None, finished=None, b_done=None, store=False):
            steps = slot_order(attn, prepared, finished)
            kind = {g: (attn if g < G else prepared) for g in range(G + 3)}
            scores = [s for s in steps if s[0] == "score"]
            values = [s for s in steps if s[0] == "values"]
            rings = [s for s in steps if s[0] in ("max", "turn", "out")]
            nth_bank = {s: i for i, s in enumerate(s for s in steps if s[0] in RING_STEPS)}
            banked = list(nth_bank)
            BY_SCALAR = ("p_turn", "p_qk", "p_v", "m_aturn", "m_yturn")
            BY_VECTOR = ("p_sum", "p_spread", "m_ao", "m_gate", "m_up", "m_down", "m_out")
            work = [s for s in steps if s[0] in BY_SCALAR + BY_VECTOR]
            by_scalar = [s for s in work if s[0] in BY_SCALAR]
            by_vector = [s for s in work if s[0] in BY_VECTOR]
            stacks = [s for s in steps if s[0] == "stack"]
            turns = [s for s in steps if s[0] == "turn"]
            v_copies = [s for s in steps if s[0] == "v_copy"]
            nth_score = {s: i + 1 for i, s in enumerate(scores)}
            nth_value = {s: i + 1 for i, s in enumerate(values)}
            nth_ring = {s: i + 1 for i, s in enumerate(rings)}
            nth_work = {s: i + 1 for i, s in enumerate(work)}
            nth_scalar = {s: i + 1 for i, s in enumerate(by_scalar)}
            nth_split = {s: i + 1 for odd in (0, 1)
                         for i, s in enumerate(s for s in steps if s[0] == "p_split" and s[3] % 2 == odd)}
            nth_vector = {s: i + 1 for i, s in enumerate(by_vector)}
            pcs = pieces(attn) if attn is not None else []
            last_max = {s[1]: nth_ring[s] for s in rings if s[0] == "max"}
            YT_READERS = [("m_up", "e1u", 1)]

            def diagonal(piece):
                return attn and piece[2] == piece[0] * P

            nth_diag, count = {}, 0
            for s in scores:
                count += bool(diagonal(s[3]))
                nth_diag[s] = count

            def ring_bank(s):
                return bank(HALVES + nth_bank[s] % RING)

            def exps(s):
                return EXPS[:, nth_value[("values", s[1], s[-1])] % PIECES, :, :]

            def half_cols(h):
                return slice(h * BANK, (h + 1) * BANK)

            with nc.Block() as block:
                @block.tensor
                def _(pe):
                    def ring_slot(s):
                        if nth_bank[s] >= RING:
                            old = banked[nth_bank[s] - RING]
                            if old in nth_score:
                                pe.wait_ge(sm["s_exp"], nth_score[old])
                            elif old in nth_ring:
                                pe.wait_ge(sm["v_ring"], nth_ring[old])
                            elif old in nth_scalar:
                                pe.wait_ge(sm["s_work"], nth_scalar[old])
                            else:
                                pe.wait_ge(sm["v_work"], nth_vector[old])
                        return ring_bank(s)

                    def turn4(to, source):
                        for t in range(4):
                            last = pe.transpose(to[:, t * P:(t + 1) * P], source(t), ident[:, :])
                        return last

                    for s in steps:
                        if s[0] == "max":
                            _, g, j, qt, lo, hi = s
                            to, h = ring_slot(s), 4 * (g % G) + j
                            if j == 0 and lo == 0 and s == next(r for r in rings if r[:2] == s[:2]):
                                if ("stack", g) in stacks:
                                    pe.wait_ge(sm[f"d_stack{g}"], STACKED)
                            tail = kind[g] and hi == (qt + 1) * P
                            last = pe.matmul(to[:, 0:hi - lo], QS[:, h // 2, qt * P:(qt + 1) * P], KZ[:, h % 2, h // 2, lo:hi],
                                             start=True, stop=not tail)
                            if tail:
                                last = pe.matmul(to[:, hi - lo - P:hi - lo], identb[:, :], negmask[:, :],
                                                 start=False, stop=True)
                            last.then_inc(sm["t_ring"], 1)
                        elif s[0] == "turn":
                            to = ring_slot(s).bitcast(BF16)
                            pe.wait_ge(sm["g_split"], turns.index(s) + 1)
                            for qt in range(T):
                                last = pe.transpose(to[0:4 * NC_ROWS, qt * P:(qt + 1) * P],
                                                    CT[:, qt, :, :].rearrange("p a b -> p (a b)"), identb[:, :])
                            last.then_inc(sm["t_ring"], 1)
                        elif s[0] == "score":
                            _, g, j, (kt, half, lo, hi) = s
                            h = 4 * g + j
                            if s[3] == pcs[0] and j == 0 and g > 0:
                                pe.wait_ge(sm["d_max"], 64 * (turns.index(("turn", g)) + 1))
                            to = ring_slot(s)
                            pe.matmul(to[:, 0:hi - lo], KZ[:, h % 2, h // 2, kt * P:(kt + 1) * P], QS[:, h // 2, lo:hi],
                                      start=True, stop=True).then_inc(sm["t_scores"], 1)
                        elif s[0] == "values":
                            _, g, piece = s
                            kt, half, lo, hi = piece
                            final = max(p[0] for p in pcs if p[1] == half)
                            newest = ("score", g, 3, piece)
                            pe.wait_ge(sm["s_exp"], nth_score[newest])
                            if diagonal(piece):
                                pe.wait_ge(sm["g_diag"], nth_diag[newest])
                            if kt == 0 and g > 0:
                                pe.wait_ge(sm["s_evac"], 2 * (g - 1) + half + 1)
                            if kt == 0 and half == 0 and g == G - 1:
                                pe.wait_ge(sm["g_vcopy"], 1)
                            for j in range(4):
                                last = pe.matmul(PS[32 * j:32 * j + 32, lo:hi], V[:, kt, 4 * g + j, :],
                                                 exps(s)[:, j, lo - half * BANK:hi - half * BANK], start=(kt == 0), stop=(kt == final))
                            last.then_inc(sm["t_values"], 1)
                        elif s[0] == "out":
                            _, g, h = s
                            to = ring_slot(s)
                            pe.wait_ge(sm["s_evac"], 2 * g + h + 1)
                            turn4(to, lambda t: OT[:, (4 * h + t) * P:(4 * h + t + 1) * P]).then_inc(sm["t_ring"], 1)
                        elif s[0] == "p_turn":
                            to = ring_slot(s)
                            pe.wait_ge(sm["v_norm"], s[1] + 1)
                            turn4(to, lambda t: HN[:, t, :]).then_inc(sm["t_work"], 1)
                        elif s[0] == "p_qk":
                            _, h, w = s
                            to = ring_slot(s)
                            pe.wait_ge(sm["s_work"], nth_scalar[("p_turn", h)])
                            pe.matmul(to, wcol((("aq", "ak"), ("wq", "wk"))[prepared][w], 0, D), hT[:, :],
                                      start=True, stop=True).then_inc(sm["t_work"], 1)
                        elif s[0] == "p_v":
                            to = ring_slot(s)
                            for t in range(4):
                                last = pe.matmul(to[:, t * D:(t + 1) * D], hT[:, t * P:(t + 1) * P],
                                                 wcol(("av", "wv")[prepared], 0, D), start=True, stop=True)
                            last.then_inc(sm["t_work"], 1)
                        elif s[0] == "p_sum":
                            h, to = s[1], ring_slot(s)
                            pe.wait_ge(sm["g_square"], 2 * h + 2)
                            for w in range(2):
                                for t in range(4):
                                    at = (4 * w + t) * H
                                    last = pe.matmul(to[:, at:at + H], SQ[:, w, t * P:(t + 1) * P], headsum[:, :],
                                                     start=True, stop=True)
                            last.then_inc(sm["t_work"], 1)
                        elif s[0] == "p_spread":
                            _, h, w = s
                            to = ring_slot(s)
                            pe.wait_ge(sm["s_root"], h + 1)
                            turn4(to, lambda t: SQ[:, w, t * P:(t + 1) * P]).then_inc(sm["t_work"], 1)
                        elif s[0] == "m_aturn":
                            turn4(ring_slot(s), lambda t: AO[:, 4 * s[1] + t, :]).then_inc(sm["t_work"], 1)
                        elif s[0] in ("m_ao", "m_out"):
                            h, (name, c0) = s[1], (("wo", KEEP0) if s[0] == "m_ao" else ("ao", 0))
                            to, width = ring_slot(s), D - c0
                            pe.wait_ge(sm["s_work"], nth_scalar[("m_aturn", h)])
                            for t in range(4):
                                last = pe.matmul(to[:, t * width:(t + 1) * width],
                                                 AOT[:, (4 * h + t) * P:(4 * h + t + 1) * P], wcol(name, c0, D),
                                                 start=True, stop=True)
                            last.then_inc(sm["t_work"], 1)
                        elif s[0] == "m_yturn":
                            to = ring_slot(s)
                            pe.wait_ge(sm["g_norm"], 2 * (s[1] + 1))
                            turn4(to, lambda t: YN[:, t, :]).then_inc(sm["t_work"], 1)
                        elif s[0] == "m_gate":
                            to = ring_slot(s)
                            pe.wait_ge(sm["s_work"], nth_scalar[("m_yturn", s[1])])
                            for t in range(4):
                                last = pe.matmul(to[:, t * E:(t + 1) * E], YT[:, t * P:(t + 1) * P], wcol("gate", 0, E),
                                                 start=True, stop=True)
                            last.then_inc(sm["t_work"], 1)
                        elif s[0] == "m_up":
                            _, c, name, chunk = s
                            to = ring_slot(s)
                            src = [YT]
                            if name in ("e3b", "e2b"):
                                src = [B1[:, 0, :]] if name == "e3b" else [A1[:, 0, :], A1[:, 1, :]]
                                pe.wait_ge(sm["s_gelu"], 3 * c + 1)
                            elif name == "e2c":
                                src = [A2[:, 0, :], A2[:, 1, :]]
                                pe.wait_ge(sm["s_gelu"], 3 * c + 2)
                            for k, rows in enumerate(src):
                                at = k * FFN_HID + chunk * P
                                last = pe.matmul(to, wcol(name, at, at + P), rows,
                                                 start=(k == 0), stop=(k == len(src) - 1))
                            last.then_inc(sm["t_work"], 1)
                        elif s[0] == "m_down":
                            _, c, t = s
                            to = ring_slot(s)
                            if t == 0:
                                pe.wait_ge(sm["s_gelu"], 3 * c + 3)
                                pe.wait_ge(sm["v_work"], nth_vector[("m_up", c, "e1u", 1)])
                            for e, hidden in enumerate((H0, H1, A3, B2)):
                                for k in range(2):
                                    last = pe.matmul(to[:, e * OUTW:(e + 1) * OUTW], hidden[:, k, t * P:(t + 1) * P],
                                                     wcol(f"d{e}", k * D + KEEP0, (k + 1) * D), start=(k == 0), stop=(k == 1))
                            last.then_inc(sm["t_work"], 1)

                @block.scalar
                def _(act):
                    def copy_work(s, to, scale=1.0, view=None):
                        act.wait_ge(sm["t_work"], nth_work[s])
                        src = ring_bank(s) if view is None else view(ring_bank(s))
                        act.activation(to, src, ACT.Copy, scale=scale).then_inc(sm["s_work"], 1)

                    act.activation(EPS[:, 3:4], EPS[:, 2:3], ACT.Exp)
                    for s in steps:
                        if s[0] == "score":
                            _, g, j, (kt, half, lo, hi) = s
                            nth = nth_value[("values", g, s[3])]
                            if nth > PIECES:
                                act.wait_ge(sm["t_values"], nth - PIECES)
                            act.wait_ge(sm["t_scores"], nth_score[s])
                            act.activation(exps(s)[:, j, lo - half * BANK:hi - half * BANK], ring_bank(s)[:, 0:hi - lo], ACT.Exp)\
                               .then_inc(sm["s_exp"], 1)
                        elif s[0] == "evac":
                            g = s[1]
                            act.wait_ge(sm["t_values"], nth_value[("values", g, pcs[-1])])
                            for h in range(HALVES):
                                if g > 0:
                                    act.wait_ge(sm["t_ring"], nth_ring[("out", g - 1, h)])
                                act.activation(OT[:, half_cols(h)], bank(h), ACT.Copy).then_inc(sm["s_evac"], 1)
                        elif s[0] == "p_turn":
                            if s[1]:
                                act.wait_ge(sm["t_work"], nth_work[("p_v", s[1] - 1)])
                            copy_work(s, hT[:, :])
                        elif s[0] == "p_qk":
                            _, h, w = s
                            if h:
                                act.wait_ge(sm["g_parts"], nth_split[("p_split", h - 1, w, 1)])
                            copy_work(s, QK[:, w, :], scale=(SCALE if w == 0 and not prepared else 1.0))
                        elif s[0] == "p_v":
                            if attn is not None:
                                act.wait_ge(sm["g_vcopy"], 1)
                            copy_work(s, VS[:, 4 * s[1]:4 * s[1] + 4, :].rearrange("p t d -> p (t d)"))
                        elif s[0] == "p_root":
                            act.wait_ge(sm["v_root"], s[1] + 1)
                            act.activation(SQ[:, :, :].rearrange("p w (t a d q) -> p (w t a) d q", t=4, d=HD, q=2),
                                           ROOT[:, :, :, :].rearrange("p w t (a q) -> p (w t a) q", q=2).unsqueeze(2)
                                           .to_broadcast([P, 4 * H, HD, 2]), ACT.Sqrt).then_inc(sm["s_root"], 1)
                        elif s[0] == "p_split" and s[3] % 2 == 0:
                            _, h, w, n = s
                            if n:
                                act.wait_ge(sm["g_parts"], nth_split[("p_split", h, w, 1)])
                            elif prepared:
                                act.wait_ge(sm["v_work"], nth_vector[("p_spread", h, w)])
                            else:
                                act.wait_ge(sm["s_work"], nth_scalar[("p_qk", h, w)])
                            if h and n == 0:
                                act.wait_ge(sm[f"d_scratch{w}"], 16 * h)
                            act.activation(PARTS[:, w, n // 2, :], (SQ if n else QK)[:, w, :], ACT.Copy)\
                               .then_inc(sm["s_split"], 1)
                        elif s[0] == "m_aturn":
                            copy_work(s, AOT[:, half_cols(s[1])])
                        elif s[0] == "m_yturn":
                            if s[1]:
                                act.wait_ge(sm["t_work"], nth_work[("m_up", s[1] - 1, "e1u", 1)])
                            copy_work(s, YT)
                        elif s[0] == "m_rexp":
                            act.wait_ge(sm["v_logits"], s[1] + 1)
                            act.activation(RT[:, 4, :, :], RT[:, 3, :, :], ACT.Exp).then_inc(sm["s_rexp"], 1)
                        elif s[0] == "m_up" and s[2] == "e1g":
                            _, c, name, chunk = s
                            act.wait_ge(sm["t_work"], nth_work[s])
                            if c:
                                act.wait_ge(sm["t_work"], nth_work[("m_down", c - 1, 3)])
                            act.activation(TH[:, chunk, :], ring_bank(s), ACT.Tanh, scale=0.5).then_inc(sm["s_tanh"], 1)
                        elif s[0] == "m_gelu":
                            _, c, level = s
                            newest = (("e3a", 0), ("e2b", 1), ("e2c", 1))[level]
                            act.wait_ge(sm["v_work"], nth_vector[("m_up", c) + newest])
                            act.activation(LEVELS[level], LEVELS[level], ACT.Gelu).then_inc(sm["s_gelu"], 1)

                @block.vector
                def _(dve):
                    chain = [0]

                    def link(ins):
                        chain[0] += 1
                        ins.then_inc(sm["v_chain"], 1)
                        dve.wait_ge(sm["v_chain"], chain[0])

                    def wide(small):
                        return small.unsqueeze(2).to_broadcast([P, 4, E])

                    def x_cols(b, c):
                        return X[:, bass.ts(b * HALVES + c, BANK)]

                    for s in steps:
                        if s[0] == "max":
                            _, g, j, qt, lo, hi = s
                            if g > 1 and ("split", g - 1) in steps:
                                dve.wait_ge(sm["g_split"], turns.index(("turn", g - 1)) + 1)
                            dve.wait_ge(sm["t_ring"], nth_ring[s])
                            dve.tensor_reduce(NM[:, lo // BANK, qt, j:j + 1], ring_bank(s)[:, 0:hi - lo], AXX, ALU.max,
                                              negate=True).then_inc(sm["v_ring"], 1)
                        elif s[0] == "split":
                            dve.wait_ge(sm["v_ring"], last_max[s[1]])
                            both = slice(4 if kind[s[1]] else 0, T)
                            dve.tensor_tensor(NM[:, 0, both, :], NM[:, 0, both, :], NM[:, 1, both, :], ALU.min)\
                               .then_inc(sm["v_max"], 1)
                        elif s[0] == "turn":
                            n = turns.index(s)
                            if n:
                                dve.wait_ge(sm["d_max"], 64 * n)
                            dve.wait_ge(sm["t_ring"], nth_ring[s])
                            dve.tensor_copy(CTS[:, :], ring_bank(s).bitcast(BF16)[0:4 * NC_ROWS, 0:S])\
                               .then_inc(sm["v_ring"], 1)
                        elif s[0] == "out":
                            _, g, h = s
                            dve.wait_ge(sm["t_ring"], nth_ring[s])
                            if g == 0 and finished is not None:
                                dve.wait_ge(sm["t_work"], nth_work[("m_aturn", h)])
                            o = ring_bank(s).rearrange("p (t j c) -> p t j c", t=4, j=4)
                            if g > 0:
                                dve.wait_ge(sm["v_ring"], nth_ring[("out", g - 1, h)])
                            tiles = slice(4 * h, 4 * h + 4)
                            link(dve.reciprocal(RD[:, tiles, :], o[:, :, :, HD]))
                            dve.tensor_tensor(AO[:, tiles, 32 * g:32 * (g + 1)].rearrange("p t (j d) -> p t j d", j=4),
                                              o[:, :, :, 0:HD], RD[:, tiles, :].unsqueeze(3).to_broadcast([P, 4, 4, HD]),
                                              ALU.mult).then_inc(sm["v_ring"], 1)
                        elif s[0] == "p_stats":
                            for t in range(T):
                                last = dve.bn_stats(BST[:, t, :], X[:, bass.ts(b_prep * T + t, D)])
                            link(last)
                            for t in range(T):
                                last = dve.bn_aggr(MV[:, t, :], BST[:, t, :])
                            last.then_inc(sm["v_stats"], 1)
                            dve.wait_ge(sm["v_stats"], 1)
                            dve.tensor_copy(MVA[:, bass.ts(b_prep, 2 * T)], MV[:, :, :].rearrange("p t n -> p (t n)"))
                        elif s[0] == "p_norm":
                            h = s[1]
                            dve.wait_ge(sm["g_rr"], 1)
                            if h:
                                dve.wait_ge(sm["t_work"], nth_work[("p_turn", h - 1)])
                            for t in range(4):
                                tile = 4 * h + t
                                last = dve.tensor_scalar(HN[:, t, :], X[:, bass.ts(b_prep * T + tile, D)], MV[:, tile, 0:1],
                                                         RR[:, tile:tile + 1], ALU.subtract, ALU.mult)
                            last.then_inc(sm["v_norm"], 1)
                        elif s[0] == "p_sum":
                            dve.wait_ge(sm["t_work"], nth_work[s])
                            if s[1]:
                                dve.wait_ge(sm["s_root"], s[1])
                            dve.tensor_scalar(ROOT[:, :, :, :].rearrange("p w t h -> p (w t h)"),
                                              ring_bank(s)[:, 0:2 * 4 * H], 1.0 / HD, RMS_EPS, ALU.mult, ALU.add)\
                               .then_inc(sm["v_work"], 1)
                            dve.wait_ge(sm["v_work"], nth_vector[s])
                            dve.reciprocal(ROOT[:, :, :, :], ROOT[:, :, :, :]).then_inc(sm["v_root"], 1)
                        elif s[0] == "p_spread":
                            _, h, w = s
                            dve.wait_ge(sm["t_work"], nth_work[s])
                            dve.scalar_tensor_tensor(QK[:, w, :], QK[:, w, :], VEC[:, 2 + w:3 + w], ring_bank(s),
                                                     ALU.mult, ALU.mult).then_inc(sm["v_work"], 1)
                        elif s[0] == "m_out":
                            dve.wait_ge(sm["t_work"], nth_work[s])
                            rows = x_cols(b_done, s[1])
                            dve.tensor_tensor(rows, rows, ring_bank(s), ALU.add).then_inc(sm["v_work"], 1)
                        elif s[0] == "m_u":
                            c = s[1]
                            if c:
                                dve.wait_ge(sm["v_x"], c)
                            for t in range(4):
                                tile = 4 * c + t
                                last = dve.tensor_scalar(UM[:, t, :], X[:, bass.ts(b_done * T + tile, D)],
                                                         MVA[:, bass.ds(b_done * (2 * T) + 2 * tile, 1)],
                                                         RSTDA[:, bass.ds(b_done * T + tile, 1)], ALU.subtract, ALU.mult)
                            link(last)
                        elif s[0] == "m_ao":
                            dve.wait_ge(sm["t_work"], nth_work[s])
                            kept = UM[:, :, KEEP0:D]
                            dve.tensor_tensor(kept, kept, ring_bank(s)[:, 0:4 * OUTW].rearrange("p (t n) -> p t n", t=4),
                                              ALU.add).then_inc(sm["v_work"], 1)
                        elif s[0] == "m_rms":
                            dve.wait_ge(sm["g_msquare"], s[1] + 1)
                            dve.tensor_reduce(R2[:, :], YN[:, :, :], AXX, ALU.add).then_inc(sm["v_sums"], 1)
                        elif s[0] == "m_gate":
                            dve.wait_ge(sm["t_work"], nth_work[s])
                            dve.tensor_copy(RT[:, 0, :, :], ring_bank(s)[:, 0:4 * E].rearrange("p (t e) -> p t e", t=4))\
                               .then_inc(sm["v_work"], 1)
                        elif s[0] == "m_logits":
                            dve.wait_ge(sm["v_work"], nth_vector[("m_gate", s[1])])
                            dve.memset(RT[:, 1, :, :], 0.0)
                            link(dve.tensor_tensor(RT[:, 2, :, :].bitcast(I32), RT[:, 0, :, :], RT[:, 0, :, :], ALU.is_equal))
                            link(dve.copy_predicated(RT[:, 1, :, :], RT[:, 2, :, :].bitcast(I32), RT[:, 0, :, :]))
                            link(dve.tensor_scalar(RT[:, 1, :, :], RT[:, 1, :, :], FMAX, -FMAX, ALU.min, ALU.max))
                            link(dve.tensor_reduce(RS[:, 0, :], RT[:, 1, :, :], AXX, ALU.max))
                            dve.tensor_tensor(RT[:, 3, :, :], RT[:, 1, :, :], wide(RS[:, 0, :]), ALU.subtract)\
                               .then_inc(sm["v_logits"], 1)
                        elif s[0] == "m_route":
                            dve.wait_ge(sm["s_rexp"], s[1] + 1)
                            link(dve.tensor_reduce(RS[:, 1, :], RT[:, 4, :, :], AXX, ALU.add))
                            link(dve.reciprocal(RS[:, 1, :], RS[:, 1, :]))
                            link(dve.tensor_tensor(RT[:, 5, :, :], RT[:, 4, :, :], wide(RS[:, 1, :]), ALU.mult))
                            for j in range(E):
                                for lo, hi, op in ((0, j, ALU.is_gt), (j + 1, E, ALU.is_ge)):
                                    if lo < hi:
                                        last = dve.tensor_tensor(CMP[:, :, lo:hi, j],
                                                                 RT[:, 5, :, j:j + 1].to_broadcast([P, 4, hi - lo]),
                                                                 RT[:, 5, :, lo:hi], op)
                            link(last)
                            link(dve.tensor_reduce(RT[:, 6, :, :], CMP[:, :, :, :], AXX, ALU.add))
                            link(dve.scalar_tensor_tensor(RT[:, 8, :, :], RT[:, 6, :, :], 2.0, RT[:, 5, :, :],
                                                          ALU.is_lt, ALU.mult))
                            link(dve.tensor_reduce(RS[:, 2, :], RT[:, 8, :, :], AXX, ALU.add))
                            link(dve.tensor_scalar(RS[:, 2, :], RS[:, 2, :], 1e-8, None, ALU.add))
                            link(dve.reciprocal(RS[:, 2, :], RS[:, 2, :]))
                            link(dve.tensor_tensor(RT[:, 9, :, :], RT[:, 8, :, :], wide(RS[:, 2, :]), ALU.mult))
                        elif s[0] == "m_up":
                            _, c, name, chunk = s
                            if c and (name, chunk) in (("e0u", 0), ("e1g", 0)):
                                dve.wait_ge(sm["t_work"], nth_work[("m_down", c - 1, 3)])
                            if name == "e1g":
                                dve.wait_ge(sm["s_tanh"], 2 * c + chunk + 1)
                                dve.scalar_tensor_tensor(TH[:, chunk, :], TH[:, chunk, :], 1.0, ring_bank(s),
                                                         ALU.add, ALU.mult).then_inc(sm["v_work"], 1)
                            elif name == "e1u":
                                dve.wait_ge(sm["v_work"], nth_vector[("m_up", c, "e1g", chunk)])
                                dve.wait_ge(sm["t_work"], nth_work[s])
                                dve.scalar_tensor_tensor(H1[:, chunk, :], TH[:, chunk, :], 0.5, ring_bank(s),
                                                         ALU.mult, ALU.mult).then_inc(sm["v_work"], 1)
                            else:
                                if name == "e3b":
                                    dve.wait_ge(sm["v_work"], nth_vector[("m_up", c, "e1u", chunk)])
                                dve.wait_ge(sm["t_work"], nth_work[s])
                                raw = {"e0u": H0, "e2a": A1, "e3a": B1, "e3b": B2, "e2b": A2, "e2c": A3}[name]
                                dve.tensor_copy(raw[:, chunk, :], ring_bank(s)).then_inc(sm["v_work"], 1)
                        elif s[0] == "m_down":
                            _, c, t = s
                            dve.wait_ge(sm["t_work"], nth_work[s])
                            dve.tensor_tensor(WD[:, t % 2, :, :],
                                              ring_bank(s)[:, 0:E * OUTW].rearrange("p (e n) -> p e n", e=E),
                                              RT[:, 9, t, :].unsqueeze(2).to_broadcast([P, E, OUTW]), ALU.mult)\
                               .then_inc(sm["v_work"], 1)
                            dve.wait_ge(sm["v_work"], nth_vector[s])
                            link(dve.tensor_reduce(WS[:, t % 2, :], WD[:, t % 2, :, :].rearrange("p e n -> p n e"),
                                                   AXX, ALU.add))
                            link(dve.tensor_tensor(UM[:, t, KEEP0:D], UM[:, t, KEEP0:D], WS[:, t % 2, :], ALU.add))
                        elif s[0] == "m_x":
                            rows = x_cols(b_done, s[1])
                            dve.scalar_tensor_tensor(rows, UM[:, :, :].rearrange("p t d -> p (t d)"), 0.5, rows,
                                                     ALU.mult, ALU.add).then_inc(sm["v_x"], 1)

                @block.gpsimd
                def _(pool):
                    chain = [0]

                    def link(ins):
                        chain[0] += 1
                        ins.then_inc(sm["g_chain"], 1)
                        pool.wait_ge(sm["g_chain"], chain[0])

                    def minus_half(n):
                        return EPS[:, 4:5].to_broadcast([P, n])

                    for s in steps:
                        if s[0] == "score" and diagonal(s[3]):
                            _, g, j, (kt, half, lo, hi) = s
                            pool.wait_ge(sm["s_exp"], nth_score[s])
                            tile = exps(s)[:, j, lo - half * BANK:lo - half * BANK + P]
                            pool.affine_select(out=tile, in_=tile, compare_op=ALU.is_ge, fill=0.0, base=0,
                                               pattern=[[1, P]], channel_multiplier=-1).then_inc(sm["g_diag"], 1)
                        elif s[0] == "split":
                            g = s[1]
                            pool.wait_ge(sm["v_max"], turns.index(("turn", g)) + 1)
                            if turns.index(("turn", g)):
                                pool.wait_ge(sm["t_ring"], nth_ring[turns[turns.index(("turn", g)) - 1]])
                            link(pool.tensor_copy(CT[:, :, 0, :], NM[:, 0, :, :]))
                            link(pool.tensor_tensor(NR[:, :, :], NM[:, 0, :, :], CT[:, :, 0, :], ALU.subtract))
                            link(pool.tensor_copy(CT[:, :, 1, :], NR[:, :, :]))
                            pool.tensor_tensor(CT[:, :, 2, :], NR[:, :, :], CT[:, :, 1, :], ALU.subtract)\
                                .then_inc(sm["g_split"], 1)
                            pool.wait_ge(sm["g_split"], turns.index(("turn", g)) + 1)
                        elif s[0] == "v_copy":
                            g = s[1]
                            if g >= G:
                                pool.wait_ge(sm["s_work"], nth_scalar[("p_v", 1)])
                                if attn is not None:
                                    pool.wait_ge(sm["t_values"], nth_value[("values", g - G, pcs[-1])])
                            h0 = 4 * (g % G)
                            pool.tensor_copy(V[:, :, h0:h0 + 4, 0:HD],
                                             VS[:, :, h0 * HD:(h0 + 4) * HD].rearrange("p t (j d) -> p t j d", j=4))\
                                .then_inc(sm["g_vcopy"], 1)
                        elif s[0] == "p_stats":
                            pool.wait_ge(sm["v_stats"], 1)
                            link(pool.tensor_scalar(RR[:, :], MV[:, :, 1], LN_EPS, None, ALU.add))
                            link(pool.tensor_tensor(RSTD[:, :], RR[:, :], minus_half(T), ALU.pow))
                            if prepared:
                                link(pool.tensor_tensor(RR[:, :], MV[:, :, 1], RSTD[:, :], ALU.mult))
                                link(pool.tensor_tensor(RR[:, :], RR[:, :], RSTD[:, :], ALU.mult))
                                link(pool.tensor_scalar(RR[:, :], RR[:, :], RMS_EPS, None, ALU.add))
                                link(pool.tensor_tensor(RR[:, :], RR[:, :], minus_half(T), ALU.pow))
                                pool.tensor_tensor(RR[:, :], RR[:, :], RSTD[:, :], ALU.mult).then_inc(sm["g_rr"], 1)
                            else:
                                pool.tensor_copy(RR[:, :], RSTD[:, :]).then_inc(sm["g_rr"], 1)
                            pool.tensor_copy(RSTDA[:, bass.ts(b_prep, T)], RSTD[:, :])
                        elif s[0] == "p_square":
                            _, h, w = s
                            pool.wait_ge(sm["s_work"], nth_scalar[("p_qk", h, w)])
                            if h:
                                pool.wait_ge(sm["g_parts"], nth_split[("p_split", h - 1, w, 3)])
                            pool.tensor_tensor(SQ[:, w, :], QK[:, w, :], QK[:, w, :], ALU.mult).then_inc(sm["g_square"], 1)
                        elif s[0] == "p_split" and s[3] % 2:
                            _, h, w, n = s
                            former = QK[:, w, :] if n == 1 else SQ[:, w, :]
                            pool.wait_ge(sm["s_split"], nth_split[("p_split", h, w, n - 1)])
                            if h and n == 1:
                                pool.wait_ge(sm["g_parts"], nth_split[("p_split", h - 1, w, 3)])
                            pool.tensor_tensor(SQ[:, w, :] if n == 1 else PARTS[:, w, 2, :], former,
                                               PARTS[:, w, n // 2, :], ALU.subtract).then_inc(sm["g_parts"], 1)
                        elif s[0] == "m_square":
                            c = s[1]
                            pool.wait_ge(sm["v_work"], nth_vector[("m_ao", c)])
                            if c:
                                pool.wait_ge(sm["t_work"], nth_work[("m_yturn", c - 1)])
                            pool.tensor_tensor(YN[:, :, :], UM[:, :, :], UM[:, :, :], ALU.mult).then_inc(sm["g_msquare"], 1)
                        elif s[0] == "m_norm":
                            c = s[1]
                            pool.wait_ge(sm["v_sums"], c + 1)
                            link(pool.tensor_scalar(R2[:, :], R2[:, :], 1.0 / D, RMS_EPS, ALU.mult, ALU.add))
                            pool.tensor_tensor(R2[:, :], R2[:, :], minus_half(4), ALU.pow).then_inc(sm["g_norm"], 1)
                            pool.wait_ge(sm["g_norm"], 2 * c + 1)
                            pool.tensor_tensor(YN[:, :, :], UM[:, :, :], R2[:, :].unsqueeze(2).to_broadcast([P, 4, D]),
                                               ALU.mult).then_inc(sm["g_norm"], 1)

                @block.sync
                def _(sp):
                    for s in steps:
                        if s[0] == "stack":
                            g = s[1]
                            now = attn if g < G else prepared
                            if g >= G:
                                for w in range(2):
                                    sp.wait_ge(sm[f"d_scratch{w}"], 16 * HALVES)
                                if attn is not None:
                                    sp.wait_ge(sm["t_scores"], nth_score[("score", g - G, 3, pcs[-1])])
                            stacked, g = sm[f"d_stack{g}"], g % G
                            scr = SCR.rearrange("w s (g e d q) t -> w g e s d (q t)", g=G, e=2, d=HD)
                            for e in range(2):
                                qs = QS[:, 2 * g:2 * g + 2, :].rearrange("p q t -> p (q t)")
                                kz = KZ[:, e, 2 * g:2 * g + 2, :].rearrange("p q t -> p (q t)")
                                sp.dma_start(QS[HROWS * e + EXTRA:HROWS * (e + 1), 2 * g:2 * g + 2, :],
                                             query_rows[0 if now else 1].rearrange("r (g q e) t -> g e r q t", g=G, e=2)
                                             [g, e]).then_inc(stacked, 16)
                                at = HROWS * e
                                for part, n in ((0, 3), (1, 2), (2, 1)):
                                    sp.dma_start(qs[at:at + n * HD],
                                                 scr[0, g, e, part].unsqueeze(0).to_broadcast([n, HD, 2 * S]))\
                                      .then_inc(stacked, 16)
                                    at += n * HD
                                at = HROWS * e
                                for n in (3, 2, 1):
                                    sp.dma_start(kz[at:at + n * HD], scr[1, g, e, 0:n])\
                                      .then_inc(stacked, 16)
                                    at += n * HD
                        elif s[0] == "p_store":
                            _, h, w = s
                            if attn is not None:
                                sp.wait_ge(sm["d_stack3"], STACKED)
                            sp.wait_ge(sm["g_parts"], nth_split[("p_split", h, w, 3)])
                            sp.dma_start(SCR[w].rearrange("s p t -> p s t")[:, :, half_cols(h)], PARTS[:, w, :, :])\
                              .then_inc(sm[f"d_scratch{w}"], 16)
                        elif s[0] == "turn":
                            g = s[1] % G
                            sp.wait_ge(sm["v_ring"], nth_ring[s])
                            for j in range(4):
                                row = HROWS * (j % 2) + EXTRA
                                sp.dma_start(QS[row:row + NC_ROWS, 2 * g + j // 2, :], CTS[j:4 * NC_ROWS:4, :])\
                                  .then_inc(sm["d_max"], 16)
                        elif s[0] == "m_x" and store:
                            c = s[1]
                            sp.wait_ge(sm["v_x"], c + 1)
                            sp.dma_start(out.rearrange("b (t p) d -> p (b t) d", p=P)[:, bass.ts(b_done * HALVES + c, 4), :],
                                         X[:, bass.ts(b_done * HALVES + c, BANK)].rearrange("p (t d) -> p t d", t=4))\
                              .then_inc(sm["d_out"], 16)
                    for s in stacks:
                        sp.wait_ge(sm[f"d_stack{s[1]}"], STACKED)
                    if turns:
                        sp.wait_ge(sm["d_max"], 64 * len(turns))
                    if store and finished is not None:
                        sp.wait_ge(sm["d_out"], 16 * HALVES)

            clear(sm)

        slot(None, None, prepared=True, b_prep=0)
        for layer, ffn in enumerate((True, False, True)):
            before, after = (None, True, False)[layer], (False, True, None)[layer]
            last_layer = after is None
            slot(ffn, 0, prepared=ffn, b_prep=1, finished=before, b_done=B - 1)
            with nc.Fori(1, B - 1) as b:
                slot(ffn, b, prepared=ffn, b_prep=b + 1, finished=ffn, b_done=b - 1, store=last_layer)
            slot(ffn, B - 1, prepared=after, b_prep=0, finished=ffn, b_done=B - 2, store=last_layer)
        slot(None, None, finished=True, b_done=B - 1, store=True)


def kernel(**inputs):
    import numpy as _np
    import concourse.bacc as _bacc
    from concourse import mybir as _mybir
    from concourse.bass_utils import run_bass_kernel_spmd as _run

    a = {k: _np.asarray(v) for k, v in inputs.items()}

    def up(name):
        return a["L0_ffn_" + name].T

    def two(w):
        return _np.concatenate([w[:P], w[P:]], axis=1)

    def per_head(w):
        return _np.repeat(w.reshape(D, KV, HD), H // KV, axis=1).reshape(D, H * HD)

    at = {"wq": up("wq")[:, ROW_FEATURE], "wk": up("wk")[:, ROW_FEATURE], "wv": up("wv"), "gate": up("gate_w"), "e0u": up("e0_up"),
          "e1g": up("e1_w1"), "e1u": up("e1_w2"), "e2a": up("e2_l1"), "e3a": up("e3_down"), "wo": up("wo"),
          "e2b": two(up("e2_l2")), "e2c": two(up("e2_l3")), "e3b": up("e3_up"),
          "d0": two(up("e0_down")), "d1": two(up("e1_down")), "d2": two(up("e2_l4")), "d3": two(up("e3_out")),
          "aq": a["L0_attn_Wq"][:, ROW_FEATURE], "ak": per_head(a["L0_attn_Wk"])[:, ROW_FEATURE],
          "av": per_head(a["L0_attn_Wv"]), "ao": a["L0_attn_Wo"]}
    weights = _np.ascontiguousarray(_np.concatenate([at[name] for name, _ in WPARTS], axis=1))
    vectors = _np.ascontiguousarray(_np.stack([a["L0_ffn_n1_w"], a["L0_ffn_n2_w"], a["L0_ffn_qn_w"][ROW_FEATURE % HD],
                                               a["L0_ffn_kn_w"][ROW_FEATURE % HD]], axis=1))
    key, query = additive_rows()
    bf16 = _mybir.dt.np(_mybir.dt.bfloat16)
    key = _np.ascontiguousarray(_np.repeat(key[:, None, :], H // 2, axis=1)).astype(bf16)
    arrays = {"x": _np.ascontiguousarray(a["L0_attn_x"]), "weights": weights, "vectors": vectors,
              "head_of": (ROW_HEAD[:, None] == ROWS_HEADS).astype(_np.float32),
              "key_rows": key, "query_rows": query.astype(bf16)}

    nc = _bacc.Bacc("TRN2", target_bir_lowering=False, num_devices=1)
    args = [nc.dram_tensor(name, v.shape, _mybir.dt.from_np(v.dtype), kind="ExternalInput").ap()
            for name, v in arrays.items()]
    out = nc.dram_tensor("out", (B, S, D), FP32, kind="ExternalOutput").ap()
    macaron_kernel(nc, *args, out)
    r = _run(nc, [arrays], core_ids=[0])
    return r.results[0]["out"]
```

```python
import math
from contextlib import ExitStack

import numpy as np
import concourse.bass as bass
from concourse import mybir

FP32 = mybir.dt.float32
BF16 = mybir.dt.bfloat16
I32 = mybir.dt.int32
ALU = mybir.AluOpType
ACT = mybir.ActivationFunctionType
AXX = mybir.AxisListType.X

B, S, D = 4, 1024, 128
P = 128
T = S // P
H, HD = 16, 8
KV = 4
G = H // 4
BANK = 512
HALVES = S // BANK
FFN_HID = 256
KEEP0 = 32
OUTW = D - KEEP0
E = 4
LN_EPS = 1e-5
RMS_EPS = 1.1920929e-07
SCALE = float(np.float32(HD ** -0.5))
FMAX = float(np.finfo(np.float32).max)
MASKED = -1.0e30

QPART = (0, 0, 0, 1, 1, 2)
KPART = (0, 1, 2, 0, 1, 0)
HROWS = 64
EXTRA = HD * len(QPART)
NC_ROWS = 3
NEXTRA = HROWS - EXTRA


def f32_parts(v):
    out, rest = [], np.float32(v)
    for _ in range(3):
        bits = np.array(rest, np.float32).view(np.uint32).astype(np.uint64)
        r = ((bits + 0x7FFF + ((bits >> 16) & 1)) >> 16 << 16).astype(np.uint32).view(np.float32)
        out.append(np.float32(r))
        rest = np.float32(rest - np.float32(r))
    return out


def additive_rows():
    key = np.zeros((NEXTRA, S), np.float32)
    key[0:NC_ROWS] = 1.0
    rel = np.arange(S) - (S - 1)
    low = rel % 4
    for n in range(3):
        key[NC_ROWS + 2 * n] = rel - low
        key[NC_ROWS + 2 * n + 1] = low
    query = np.zeros((2, NEXTRA, H, S), np.float32)
    start = 2.0 ** (-2.0 ** (-(math.log2(H) - 3)))
    for h in range(H):
        for n, part in enumerate(f32_parts(np.float32(start * start ** h))):
            query[1, NC_ROWS + 2 * n, h] = part
            query[1, NC_ROWS + 2 * n + 1, h] = part
    return key, query


ROWS = [(4 * g + 2 * q + e, d) for g in range(4) for e in range(2) for d in range(HD) for q in range(2)]
ROW_FEATURE = np.array([h * HD + d for h, d in ROWS])
ROW_HEAD = np.array([h for h, _ in ROWS])
ROWS_HEADS = np.array([4 * g + 2 * q + e for g in range(4) for e in range(2) for q in range(2)])


def columns(parts):
    at, out = 0, {}
    for name, width in parts:
        out[name] = at
        at += width
    return out, at


WPARTS = [("wq", D), ("wk", D), ("wv", D),
          ("gate", E), ("e0u", 256), ("e1g", 256), ("e1u", 256), ("e2a", 256), ("e3a", 128),
          ("wo", D), ("e2b", 512), ("e2c", 512), ("e3b", 256),
          ("d0", 256), ("d1", 256), ("d2", 256), ("d3", 256),
          ("aq", D), ("ak", D), ("av", D), ("ao", D)]
WAT, WCOLS = columns(WPARTS)






def pieces(causal):
    out = []
    for kt in range(T):
        for half in range(HALVES):
            lo = max(half * BANK, kt * P if causal else 0)
            if lo < (half + 1) * BANK:
                out.append((kt, half, lo, (half + 1) * BANK))
    return out


def max_steps(g, causal):
    out = []
    for j in range(4):
        for qt in (7, 0, 6, 1, 5, 2, 4, 3):
            width = (qt + 1) * P if causal else S
            for lo in range(0, width, BANK):
                out.append(("max", g, j, qt, lo, min(lo + BANK, width)))
    return out


def prep_steps(ffn):
    out = [("p_stats",)]
    for h in range(HALVES):
        out += [("p_norm", h), ("p_turn", h), ("p_qk", h, 0), ("p_qk", h, 1), ("p_v", h)]
        if ffn:
            out += [("p_square", h, 0), ("p_square", h, 1), ("p_sum", h), ("p_root", h), ("p_spread", h, 0),
                    ("p_spread", h, 1)]
        out += [("p_split", h, w, n) for n in range(4) for w in range(2)] + [("p_store", h, 0), ("p_store", h, 1)]
    return out


UPS1 = [("e0u", 0), ("e0u", 1), ("e2a", 0), ("e2a", 1), ("e3a", 0)]
UPSG = [("e1g", 0), ("e1u", 0), ("e1g", 1), ("e1u", 1)]
UPS2 = [("e3b", 0), ("e3b", 1), ("e2b", 0), ("e2b", 1)]
UPS3 = [("e2c", 0), ("e2c", 1)]


def expert_steps(ffn, halves=range(HALVES)):
    out = [("m_aturn", h) for h in halves]
    if not ffn:
        return out + [("m_out", h) for h in range(HALVES)]
    for c in halves:
        out += [("m_u", c), ("m_ao", c), ("m_square", c), ("m_rms", c), ("m_norm", c), ("m_yturn", c), ("m_gate", c)]
        out += [("m_up", c) + u for u in UPS1]
        out += [("m_logits", c), ("m_rexp", c), ("m_gelu", c, 0), ("m_route", c)]
        out += [("m_up", c) + u for u in UPSG + UPS2] + [("m_gelu", c, 1)]
        out += [("m_up", c) + u for u in UPS3] + [("m_gelu", c, 2)]
        out += [("m_down", c, t) for t in range(4)] + [("m_x", c)]
    return out


def step_cost(s, causal):
    kind = s[0]
    fp32 = 0.86
    if kind == "max":
        n = s[5] - s[4]
        return [("pe", 0.015 + n / 2400 + (0.07 if causal and s[5] == (s[3] + 1) * P else 0)), ("dve", 0.07 + n / 960)]
    if kind == "score":
        lo, hi = s[3][2:]
        diagonal = causal and lo == s[3][0] * P
        return [("pe", 0.015 + (hi - lo) / 2400), ("act", 0.05 + (hi - lo) / 1180)] + [("pool", 0.4)] * bool(diagonal)
    if kind == "values":
        return [("pe", 0.04 + 0.92 * (s[2][3] - s[2][2]) / BANK)]
    return {
        "split": [("dve", 0.2), ("pool", 2.2)], "turn": [("pe", 0.5), ("dve", 1.2), ("sp", 2.2), ("wire", 2.0)],
        "evac": [("act", 1.05)], "out": [("pe", 0.43), ("dve", 0.6)],
        "stack": [("sp", 10.5), ("wire", 2.0)], "v_copy": [("pool", 2.0)],
        "p_stats": [("dve", 3.0), ("pool", 5.0)], "p_norm": [("dve", 0.8)], "p_turn": [("pe", 0.43), ("act", 0.5)],
        "p_qk": [("pe", fp32), ("act", 0.5)], "p_v": [("pe", fp32), ("act", 0.5)], "p_square": [("pool", 1.3)],
        "p_sum": [("pe", 1.0), ("dve", 1.1)], "p_root": [("act", 3.5)],
        "p_spread": [("pe", 0.43), ("dve", 0.7)],
        "p_split": [("pool", 1.3) if s[-1] in (1, 3) else ("act", 0.5)], "p_store": [("sp", 0.6), ("wire", 2.0)],
        "m_aturn": [("pe", 0.43), ("act", 0.5)], "m_out": [("pe", fp32), ("dve", 0.7)], "m_u": [("dve", 0.8)],
        "m_ao": [("pe", 0.75), ("dve", 0.6)], "m_square": [("pool", 1.3)], "m_rms": [("dve", 0.6)],
        "m_norm": [("pool", 2.3)], "m_yturn": [("pe", 0.43), ("act", 0.5)], "m_gate": [("pe", 0.45), ("dve", 0.15)],
        "m_logits": [("dve", 0.9)], "m_rexp": [("act", 0.2)], "m_route": [("dve", 2.5)],
        "m_up": [("pe", fp32 * (2 if s[2:3] in (("e2b",), ("e2c",)) else 1))] + [("act", 0.5)] * (s[2:3] == ("e1g",))
                + [("dve", 0.7)],
        "m_gelu": [("act", (4.7, 4.3, 3.5)[s[-1]] if kind == "m_gelu" else 0)],
        "m_down": [("pe", 1.55), ("dve", 1.5)], "m_x": [("dve", 0.6), ("sp", 0.6)],
    }[kind]


RING_STEPS = ("max", "score", "turn", "out", "p_turn", "p_qk", "p_v", "p_sum", "p_spread", "m_aturn", "m_ao", "m_out",
              "m_yturn", "m_gate", "m_up", "m_down")
PIECES = 4
RING = 6


def search_order(attn, prepared, finished, idle_act, idle_dve, late_price, slack, shift):
    pcs = pieces(attn) if attn is not None else []
    kind = {g: (attn if g < G else prepared) for g in range(G + 3)}
    streams = []

    def stream(name, steps, until):
        if steps:
            streams.append((name, steps, until))

    groups = range(G) if attn is not None else ()
    maxed = [g for g in range(1 if attn is not None else 4, 5) if kind[g] is not None]
    stream("scores", [("score", g, j, piece) for g in groups for piece in pcs for j in range(4)], 0.99)
    stream("values", [s for g in groups for s in [("values", g, piece) for piece in pcs] + [("evac", g)]], 1.0)
    stream("outs", [("out", g, h) for g in groups for h in range(HALVES)], 1.0)
    stream("maxima", [s for g in maxed for s in max_steps(g, kind[g]) + [("split", g), ("turn", g)]], 0.92)
    if attn is None and finished:
        for c in range(HALVES):
            stream("experts", expert_steps(finished, [c]), 1.0)
    else:
        stream("experts", expert_steps(finished) if finished is not None else [], 0.93)
    stream("projections", prep_steps(prepared) if prepared is not None else [], 0.45)
    loads = ([3] if attn is not None else []) + ([4, 5, 6] if prepared is not None else [])
    stream("stacks", [("stack", g) for g in loads], 0.0)
    stream("v_copies", [("v_copy", g) for g in loads], 0.0)

    def needs(s):
        k, g = s[0], s[1] if len(s) > 1 else None
        if k == "max":
            return [("stack", g)] if g in loads else []
        if k == "score":
            _, g, j, (kt, half, lo, hi) = s
            out = [("turn", g)] if g > 0 else []
            n = pcs.index(s[3]) - PIECES
            return out + ([("values", g, pcs[n])] if n >= 0 else [("values", g - 1, pcs[n])] if g > 0 else [])
        if k == "values":
            out = [("score", g, 3, s[2])]
            if s[2][0] == 0 and g > 0:
                out += [("evac", g - 1)]
            return out + ([("v_copy", 3)] if g == G - 1 and s[2][0] == 0 else [])
        if k == "evac":
            return [("out", g - 1, 1)] if g > 0 else []
        if k == "out":
            return [("evac", g)] + ([("m_aturn", s[2])] if finished is not None else [])
        if k == "stack" and g >= G:
            return [("p_store", 1, 1)] + ([("score", g - G, 3, pcs[-1])] if attn is not None else [])
        if k == "v_copy" and g >= G:
            return [("p_v", 1)] + ([("values", g - G, pcs[-1])] if attn is not None else [])
        if k == "p_v":
            return [("v_copy", 3)] if attn is not None else []
        if k == "p_store":
            return [("stack", 3)] if attn is not None else []
        return []

    waits_for = {"m_ao": ("m_u", "m_aturn"), "m_rms": ("m_square",), "m_norm": ("m_rms",), "m_yturn": ("m_norm",),
                 "m_gate": ("m_yturn",), "m_square": ("m_ao",), "m_logits": ("m_gate",), "m_rexp": ("m_logits",),
                 "m_route": ("m_rexp",), "m_out": ("m_aturn",), "p_norm": ("p_stats",), "p_turn": ("p_norm",),
                 "p_qk": ("p_turn",), "p_v": ("p_turn",), "p_square": ("p_qk",), "p_sum": ("p_square",),
                 "p_root": ("p_sum",), "p_spread": ("p_root",), "p_split": ("p_spread", "p_qk", "p_split"),
                 "p_store": ("p_split",),
                 "split": ("max",), "turn": ("split",), "m_down": ("m_gelu",), "evac": ("values",)}

    def needs_own(s):
        if s[0] == "m_up":
            return ("m_gelu",) if s[2] in ("e3b", "e2b", "e2c") else ("m_yturn",)
        if s[0] == "m_gelu":
            return ("m_up",)
        return waits_for.get(s[0], ())

    steps = [s for _, part, _ in streams for s in part]
    number = {s: n for n, s in enumerate(steps)}
    first = [number[part[0]] for _, part, _ in streams]
    end = [number[part[-1]] + 1 for _, part, _ in streams]
    costs = [[(ENGINES.index(e), cost) for e, cost in step_cost(s, kind.get(s[1]) if s[0] in ("max", "score") else None)]
             for s in steps]
    work = [sum(cost for c in costs for e, cost in c if e == n) for n in range(len(ENGINES))]
    needed, due = [], []
    for name, part, until in streams:
        newest = {}
        for n, s in enumerate(part):
            needed.append([number[m] for m in needs(s)] + [newest[k] for k in needs_own(s) if k in newest])
            due.append(work[0] * until * n / len(part) + shift.get(name, 0.0))
            newest[s[0]] = number[s]
    loads_only = [ENGINES[c[0][0]] in ("sp", "pool") for c in costs]

    def extended(state):
        _, at, clock, busy, done, ring, plan = state
        found = []
        for k, n in enumerate(at):
            if n == end[k] or any(done[m] is None for m in needed[n]):
                continue
            ready = max([done[m] for m in needed[n]] + [0.0])
            after, used = list(clock), list(busy)
            early = loads_only[n] and max(ready, clock[costs[n][0][0]]) > clock[0] + 0.5
            if steps[n][0] in RING_STEPS and len(ring) == RING:
                ready = max(ready, ring[0])
            for e, cost in costs[n]:
                start = max(ready, after[e])
                if ENGINES[e] != "wire":
                    after[e] = start + cost
                used[e] += cost
                ready = start + cost + SIGNAL
            found.append((loads_only[n] and not early, early, k, n, after, used, ready))
        chosen = [f for f in found if f[0]][:1] or [f for f in found if not f[1]] or [min(found, key=lambda f: f[6])]
        out = []
        for _, _, k, n, after, used, ready in chosen:
            now = used[0]
            late = sum(max(0.0, now - due[m] - slack) for q, m in enumerate(at[:k] + (n + 1,) + at[k + 1:]) if m < end[q])
            price = (1 + 0.02) * (after[0] - now) + late_price * late
            for e, weight in ((1, idle_act), (2, idle_dve)):
                price += weight * (max(after[e], after[0]) - used[e] - (work[0] - work[e]) * now / work[0])
            out.append((price, at[:k] + (n + 1,) + at[k + 1:], after, used, done,
                        (ring + (ready,))[-RING:] if steps[n][0] in RING_STEPS else ring, (plan, n, ready)))
        return out

    states = [(0.0, tuple(first), [0.0] * len(ENGINES), [0.0] * len(ENGINES), [None] * len(steps), (), None)]
    for _ in steps:
        best = {}
        for state in states:
            for new in extended(state):
                if new[1] not in best or new[0] < best[new[1]][0]:
                    best[new[1]] = new
        states = []
        for price, at, clock, busy, done, ring, plan in sorted(best.values(), key=lambda p: p[0])[:PLANS]:
            done = list(done)
            done[plan[1]] = plan[2]
            states.append((price, at, clock, busy, done, ring, plan))
    state = min(states, key=lambda p: max(p[2][:3]))
    order, plan = [], state[6]
    while plan is not None:
        plan, n, _ = plan
        order.append(steps[n])
    return order[::-1], max(state[2][:3])


def slot_order(attn, prepared, finished):
    found = [search_order(attn, prepared, finished, *weights) for weights in SEARCHES]
    return min(found, key=lambda f: f[1])[0]


ENGINES = ("pe", "act", "dve", "pool", "sp", "wire")
SIGNAL = 0.2
PLANS = 64
SEARCHES = [(0.5, 1.1, 0.003, 8.0, {"maxima": -10.0, "values": 2.0, "projections": -5.0}),
            (0.2, 0.7, 0.003, 15.0, {"maxima": -20.0, "values": 2.0, "projections": -5.0}),
            (0.2, 0.7, 0.003, 2.0, {"maxima": -20.0, "values": 0.0, "projections": -5.0}),
            (0.5, 0.9, 0.001, 4.0, {"maxima": -5.0, "values": 2.0, "projections": 0.0}),
            (0.2, 0.3, 0.01, 15.0, {"maxima": 0.0, "values": 2.0, "projections": -20.0})]


class ExpertTiles:

    def __init__(self, hidden, um, yn, r2, rt, rs, cmp_):
        self.H0, self.A1, self.B1, self.B2 = hidden[:, 0:2], hidden[:, 2:4], hidden[:, 4:5], hidden[:, 5:7]
        self.A2, self.H1, self.YT = hidden[:, 7:9], hidden[:, 9:11], hidden[:, 11, :]
        self.A3, self.TH = self.A1, self.B2
        self.LEVELS = [hidden[:, 0:5], hidden[:, 5:9], hidden[:, 2:4]]
        self.UM, self.YN, self.R2, self.RT, self.RS, self.CMP = um, yn, r2, rt, rs, cmp_


def macaron_kernel(nc, x, weights, vectors, head_of, key_rows, query_rows, out):
    ctx = ExitStack()
    with ctx:
        def sb(name, shape, dt):
            return ctx.enter_context(nc.sbuf_tensor(name, shape, dt))

        def sem(name):
            return ctx.enter_context(nc.semaphore(name))

        X = sb("X", [P, B * T * D], FP32)
        W = sb("W", [P, WCOLS], FP32)
        VEC = sb("VEC", [P, 4], FP32)
        EPS = sb("EPS", [P, 5], FP32)
        ident = sb("ident", [P, P], FP32)
        identb = sb("identb", [P, P], BF16)
        negmask = sb("negmask", [P, P], BF16)
        headsum = sb("headsum", [P, H], FP32)
        QS = sb("QS", [P, H // 2, S], BF16)
        KZ = sb("KZ", [P, 2, H // 2, S], BF16)
        V = sb("V", [P, T, H, 32], FP32)
        EXPS = sb("EXPS", [P, PIECES, 4, BANK], FP32)
        NM = sb("NM", [P, 2, T, 4], FP32)
        NR = sb("NR", [P, T, 4], FP32)
        CT = sb("CT", [P, T, NC_ROWS, 4], BF16)
        CTS = sb("CTS", [NC_ROWS * 4, S], BF16)
        OT = sb("OT", [P, S], FP32)
        RD = sb("RD", [P, T, 4], FP32)
        AO = sb("AO", [P, T, D], FP32)
        BST = sb("BST", [P, T, 6], FP32)
        MV = sb("MV", [P, T, 2], FP32)
        RSTD = sb("RSTD", [P, T], FP32)
        RR = sb("RR", [P, T], FP32)
        MVA = sb("MVA", [P, B * T * 2], FP32)
        RSTDA = sb("RSTDA", [P, B * T], FP32)
        HN = sb("HN", [P, 4, D], FP32)
        hT = sb("hT", [P, BANK], FP32)
        QK = sb("QK", [P, 2, BANK], FP32)
        SQ = sb("SQ", [P, 2, BANK], FP32)
        ROOT = sb("ROOT", [P, 2, 4, H], FP32)
        PARTS = sb("PARTS", [P, 2, 3, BANK], BF16)
        VS = sb("VS", [P, T, D], FP32)
        SCR = nc.dram_tensor("scratch_parts", [2, 3, P, S], BF16).ap()
        HID = sb("HID", [P, 12, BANK], FP32)
        AOT = sb("AOT", [P, S], FP32)
        UM = sb("UM", [P, 4, D], FP32)
        YN = sb("YN", [P, 4, D], FP32)
        R2 = sb("R2", [P, 4], FP32)
        RT = sb("RT", [P, 10, 4, E], FP32)
        RS = sb("RS", [P, 3, 4], FP32)
        CMP = sb("CMP", [P, 4, E, E], FP32)

        main_tiles = ExpertTiles(HID, UM, YN, R2, RT, RS, CMP)
        EX = EXPS[:, :, :, :].rearrange("p a b c -> p (a b c)")
        cuts = np.cumsum([0, 12 * BANK, 4 * D, 4 * D, 4, 10 * 4 * E, 3 * 4, 4 * E * E]).tolist()
        hid, um, yn, r2, rt, rs, cmp_ = [EX[:, lo:hi] for lo, hi in zip(cuts, cuts[1:])]
        second_tiles = ExpertTiles(hid.rearrange("p (n c) -> p n c", n=12), um.rearrange("p (t d) -> p t d", t=4),
                                    yn.rearrange("p (t d) -> p t d", t=4), r2,
                                    rt.rearrange("p (n t e) -> p n t e", n=10, t=4),
                                    rs.rearrange("p (n t) -> p n t", n=3),
                                    cmp_.rearrange("p (t i j) -> p t i j", t=4, i=E))
        WD = sb("WD", [P, 2, E, OUTW], FP32)
        WS = sb("WS", [P, 2, OUTW], FP32)

        PS = ctx.enter_context(nc.psum_tensor("PS", [P, 8 * BANK], FP32))

        def bank(n, width=BANK):
            return PS[:, n * BANK:n * BANK + width]

        def wcol(name, a=0, b=None):
            return W[:, WAT[name] + a:WAT[name] + b]

        loaded, loaded_late, drawn = sem("loaded"), sem("loaded_late"), sem("drawn")
        x_source = x.rearrange("b (t p) d -> p (b t) d", p=P)
        x_tiles = X[:, :].rearrange("p (n d) -> p n d", d=D)

        def clear(sems):
            for s in sems.values():
                nc.sync.sem_clear(s)
            nc.all_engine_barrier()

        with nc.Block() as block:
            @block.sync
            def _(sp):
                sp.dma_start(x_tiles[:, 0:T], x_source[:, 0:T]).then_inc(loaded, 16)
                sp.dma_start(VEC[:, :], vectors).then_inc(loaded, 16)
                sp.dma_start(W[:, 0:WAT["gate"]], weights[:, 0:WAT["gate"]]).then_inc(loaded, 16)
                sp.dma_start(headsum[:, :], head_of).then_inc(loaded, 16)
                for e in range(2):
                    rows = slice(HROWS * e + EXTRA, HROWS * (e + 1))
                    sp.dma_start(KZ[rows, e, :, :], key_rows).then_inc(loaded, 16)
                sp.dma_start(x_tiles[:, T:], x_source[:, T:]).then_inc(loaded_late, 16)
                sp.dma_start(W[:, WAT["gate"]:], weights[:, WAT["gate"]:]).then_inc(loaded_late, 16)
                sp.wait_ge(loaded, 16 * 6)

            @block.vector
            def _(dve):
                for n, value in enumerate((LN_EPS, RMS_EPS, 0.0, 0.0, -0.5)):
                    dve.memset(EPS[:, n:n + 1], value)
                dve.memset(V[:, :, :, HD:HD + 1], 1.0)
                dve.memset(V[:, :, :, HD + 1:], 0.0)
                dve.memset(CMP[:, :, :, :], 0.0)
                dve.memset(KZ[HROWS:, 0, :, :].bitcast(I32), 0)
                dve.wait_ge(loaded, 16 * 6)
                dve.tensor_scalar(W[:, 0:WAT["gate"]], W[:, 0:WAT["gate"]], VEC[:, 0:1], None, ALU.mult)
                dve.tensor_scalar(VEC[:, 2:3], VEC[:, 2:3], SCALE, None, ALU.mult)

            @block.gpsimd
            def _(pool):
                pool.memset(KZ[0:HROWS, 1, :, :].bitcast(I32), 0)
                pool.memset(ident[:, :], 0.0).then_inc(drawn, 1)
                pool.memset(identb[:, :], 0.0).then_inc(drawn, 1)
                pool.memset(negmask[:, :], 0.0).then_inc(drawn, 1)
                pool.wait_ge(drawn, 3)
                for m in (ident, identb):
                    pool.affine_select(out=m[:, :], in_=m[:, :], compare_op=ALU.not_equal, fill=1.0, base=0,
                                       pattern=[[-1, P]], channel_multiplier=1).then_inc(drawn, 1)
                pool.affine_select(out=negmask[:, :], in_=negmask[:, :], compare_op=ALU.is_ge, fill=MASKED, base=0,
                                   pattern=[[-1, P]], channel_multiplier=1).then_inc(drawn, 1)

        SEMS = ("t_scores", "t_values", "t_ring", "t_work",
                "s_exp", "s_evac", "s_work", "s_tanh", "s_gelu", "s_rexp", "s_root", "s_split",
                "v_ring", "v_max", "v_work", "v_chain", "v_stats", "v_norm", "v_root", "v_sums", "v_logits", "v_x",
                "g_chain", "g_diag", "g_split", "g_rr", "g_square", "g_parts", "g_msquare", "g_norm", "g_vcopy",
                "d_max", "d_stack3", "d_stack4", "d_stack5", "d_stack6", "d_scratch0", "d_scratch1", "d_out")
        sm = {n: sem(n) for n in SEMS}
        STACKED = 16 * 2 * (1 + 3 + 3)

        def slot(attn, b_attn, prepared=None, b_prep=None, finished=None, b_done=None, store=False, first=False):
            steps = slot_order(attn, prepared, finished)
            kind = {g: (attn if g < G else prepared) for g in range(G + 3)}
            scores = [s for s in steps if s[0] == "score"]
            values = [s for s in steps if s[0] == "values"]
            rings = [s for s in steps if s[0] in ("max", "turn", "out")]
            nth_bank = {s: i for i, s in enumerate(s for s in steps if s[0] in RING_STEPS)}
            banked = list(nth_bank)
            BY_SCALAR = ("p_turn", "p_qk", "p_v", "m_aturn", "m_yturn")
            BY_VECTOR = ("p_sum", "p_spread", "m_ao", "m_gate", "m_up", "m_down", "m_out")
            work = [s for s in steps if s[0] in BY_SCALAR + BY_VECTOR]
            by_scalar = [s for s in work if s[0] in BY_SCALAR]
            by_vector = [s for s in work if s[0] in BY_VECTOR]
            stacks = [s for s in steps if s[0] == "stack"]
            turns = [s for s in steps if s[0] == "turn"]
            nth_score = {s: i + 1 for i, s in enumerate(scores)}
            nth_value = {s: i + 1 for i, s in enumerate(values)}
            nth_ring = {s: i + 1 for i, s in enumerate(rings)}
            nth_work = {s: i + 1 for i, s in enumerate(work)}
            nth_scalar = {s: i + 1 for i, s in enumerate(by_scalar)}
            nth_split = {s: i + 1 for odd in (0, 1)
                         for i, s in enumerate(s for s in steps if s[0] == "p_split" and s[3] % 2 == odd)}
            nth_vector = {s: i + 1 for i, s in enumerate(by_vector)}
            pcs = pieces(attn) if attn is not None else []
            nth_tanh = {s: i + 1 for i, s in enumerate(s for s in steps if s[0] == "m_up" and s[2] == "e1g")}
            nth_of_kind = {s: sum(r[0] == s[0] for r in steps[:i + 1]) for i, s in enumerate(steps)}
            apart = attn is None and finished is True
            last_max = {s[1]: nth_ring[s] for s in rings if s[0] == "max"}
            YT_READERS = [("m_up", "e1u", 1)]

            def diagonal(piece):
                return attn and piece[2] == piece[0] * P

            nth_diag, count = {}, 0
            for s in scores:
                count += bool(diagonal(s[3]))
                nth_diag[s] = count

            def ring_bank(s):
                return bank(HALVES + nth_bank[s] % RING)

            def exps(s):
                return EXPS[:, nth_value[("values", s[1], s[-1])] % PIECES, :, :]

            def tiles_of(s):
                return second_tiles if apart and s[1:2] == (1,) else main_tiles

            def half_cols(h):
                return slice(h * BANK, (h + 1) * BANK)

            with nc.Block() as block:
                @block.tensor
                def _(pe):
                    def ring_slot(s):
                        if nth_bank[s] >= RING:
                            old = banked[nth_bank[s] - RING]
                            if old in nth_score:
                                pe.wait_ge(sm["s_exp"], nth_score[old])
                            elif old in nth_ring:
                                pe.wait_ge(sm["v_ring"], nth_ring[old])
                            elif old in nth_scalar:
                                pe.wait_ge(sm["s_work"], nth_scalar[old])
                            else:
                                pe.wait_ge(sm["v_work"], nth_vector[old])
                        return ring_bank(s)

                    def turn4(to, source):
                        for t in range(4):
                            last = pe.transpose(to[:, t * P:(t + 1) * P], source(t), ident[:, :])
                        return last

                    for s in steps:
                        m = tiles_of(s)
                        if s[0] == "max":
                            _, g, j, qt, lo, hi = s
                            to, h = ring_slot(s), 4 * (g % G) + j
                            if j == 0 and lo == 0 and s == next(r for r in rings if r[:2] == s[:2]):
                                if ("stack", g) in stacks:
                                    pe.wait_ge(sm[f"d_stack{g}"], STACKED)
                            tail = kind[g] and hi == (qt + 1) * P
                            last = pe.matmul(to[:, 0:hi - lo], QS[:, h // 2, qt * P:(qt + 1) * P], KZ[:, h % 2, h // 2, lo:hi],
                                             start=True, stop=not tail)
                            if tail:
                                last = pe.matmul(to[:, hi - lo - P:hi - lo], identb[:, :], negmask[:, :],
                                                 start=False, stop=True)
                            last.then_inc(sm["t_ring"], 1)
                        elif s[0] == "turn":
                            to = ring_slot(s).bitcast(BF16)
                            pe.wait_ge(sm["g_split"], turns.index(s) + 1)
                            for qt in range(T):
                                last = pe.transpose(to[0:4 * NC_ROWS, qt * P:(qt + 1) * P],
                                                    CT[:, qt, :, :].rearrange("p a b -> p (a b)"), identb[:, :])
                            last.then_inc(sm["t_ring"], 1)
                        elif s[0] == "score":
                            _, g, j, (kt, half, lo, hi) = s
                            h = 4 * g + j
                            if s[3] == pcs[0] and j == 0 and g > 0:
                                pe.wait_ge(sm["d_max"], 64 * (turns.index(("turn", g)) + 1))
                            to = ring_slot(s)
                            pe.matmul(to[:, 0:hi - lo], KZ[:, h % 2, h // 2, kt * P:(kt + 1) * P], QS[:, h // 2, lo:hi],
                                      start=True, stop=True).then_inc(sm["t_scores"], 1)
                        elif s[0] == "values":
                            _, g, piece = s
                            kt, half, lo, hi = piece
                            final = max(p[0] for p in pcs if p[1] == half)
                            newest = ("score", g, 3, piece)
                            pe.wait_ge(sm["s_exp"], nth_score[newest])
                            if diagonal(piece):
                                pe.wait_ge(sm["g_diag"], nth_diag[newest])
                            if kt == 0 and g > 0:
                                pe.wait_ge(sm["s_evac"], 2 * (g - 1) + half + 1)
                            if kt == 0 and half == 0 and g == G - 1:
                                pe.wait_ge(sm["g_vcopy"], 1)
                            for j in range(4):
                                last = pe.matmul(PS[32 * j:32 * j + 32, lo:hi], V[:, kt, 4 * g + j, :],
                                                 exps(s)[:, j, lo - half * BANK:hi - half * BANK], start=(kt == 0), stop=(kt == final))
                            last.then_inc(sm["t_values"], 1)
                        elif s[0] == "out":
                            _, g, h = s
                            to = ring_slot(s)
                            pe.wait_ge(sm["s_evac"], 2 * g + h + 1)
                            turn4(to, lambda t: OT[:, (4 * h + t) * P:(4 * h + t + 1) * P]).then_inc(sm["t_ring"], 1)
                        elif s[0] == "p_turn":
                            to = ring_slot(s)
                            pe.wait_ge(sm["v_norm"], s[1] + 1)
                            turn4(to, lambda t: HN[:, t, :]).then_inc(sm["t_work"], 1)
                        elif s[0] == "p_qk":
                            _, h, w = s
                            to = ring_slot(s)
                            pe.wait_ge(sm["s_work"], nth_scalar[("p_turn", h)])
                            pe.matmul(to, wcol((("aq", "ak"), ("wq", "wk"))[prepared][w], 0, D), hT[:, :],
                                      start=True, stop=True).then_inc(sm["t_work"], 1)
                        elif s[0] == "p_v":
                            to = ring_slot(s)
                            for t in range(4):
                                last = pe.matmul(to[:, t * D:(t + 1) * D], hT[:, t * P:(t + 1) * P],
                                                 wcol(("av", "wv")[prepared], 0, D), start=True, stop=True)
                            last.then_inc(sm["t_work"], 1)
                        elif s[0] == "p_sum":
                            h, to = s[1], ring_slot(s)
                            pe.wait_ge(sm["g_square"], 2 * h + 2)
                            for w in range(2):
                                for t in range(4):
                                    at = (4 * w + t) * H
                                    last = pe.matmul(to[:, at:at + H], SQ[:, w, t * P:(t + 1) * P], headsum[:, :],
                                                     start=True, stop=True)
                            last.then_inc(sm["t_work"], 1)
                        elif s[0] == "p_spread":
                            _, h, w = s
                            to = ring_slot(s)
                            pe.wait_ge(sm["s_root"], h + 1)
                            turn4(to, lambda t: SQ[:, w, t * P:(t + 1) * P]).then_inc(sm["t_work"], 1)
                        elif s[0] == "m_aturn":
                            turn4(ring_slot(s), lambda t: AO[:, 4 * s[1] + t, :]).then_inc(sm["t_work"], 1)
                        elif s[0] in ("m_ao", "m_out"):
                            h, (name, c0) = s[1], (("wo", KEEP0) if s[0] == "m_ao" else ("ao", 0))
                            to, width = ring_slot(s), D - c0
                            pe.wait_ge(sm["s_work"], nth_scalar[("m_aturn", h)])
                            for t in range(4):
                                last = pe.matmul(to[:, t * width:(t + 1) * width],
                                                 AOT[:, (4 * h + t) * P:(4 * h + t + 1) * P], wcol(name, c0, D),
                                                 start=True, stop=True)
                            last.then_inc(sm["t_work"], 1)
                        elif s[0] == "m_yturn":
                            to = ring_slot(s)
                            pe.wait_ge(sm["g_norm"], 2 * nth_of_kind[("m_norm", s[1])])
                            turn4(to, lambda t: m.YN[:, t, :]).then_inc(sm["t_work"], 1)
                        elif s[0] == "m_gate":
                            to = ring_slot(s)
                            pe.wait_ge(sm["s_work"], nth_scalar[("m_yturn", s[1])])
                            for t in range(4):
                                last = pe.matmul(to[:, t * E:(t + 1) * E], m.YT[:, t * P:(t + 1) * P], wcol("gate", 0, E),
                                                 start=True, stop=True)
                            last.then_inc(sm["t_work"], 1)
                        elif s[0] == "m_up":
                            _, c, name, chunk = s
                            to = ring_slot(s)
                            src = [m.YT]
                            if name in ("e3b", "e2b"):
                                src = [m.B1[:, 0, :]] if name == "e3b" else [m.A1[:, 0, :], m.A1[:, 1, :]]
                                pe.wait_ge(sm["s_gelu"], nth_of_kind[("m_gelu", c, 0)])
                            elif name == "e2c":
                                src = [m.A2[:, 0, :], m.A2[:, 1, :]]
                                pe.wait_ge(sm["s_gelu"], nth_of_kind[("m_gelu", c, 1)])
                            for k, rows in enumerate(src):
                                at = k * FFN_HID + chunk * P
                                last = pe.matmul(to, wcol(name, at, at + P), rows,
                                                 start=(k == 0), stop=(k == len(src) - 1))
                            last.then_inc(sm["t_work"], 1)
                        elif s[0] == "m_down":
                            _, c, t = s
                            to = ring_slot(s)
                            if t == 0:
                                pe.wait_ge(sm["s_gelu"], nth_of_kind[("m_gelu", c, 2)])
                                pe.wait_ge(sm["v_work"], nth_vector[("m_up", c, "e1u", 1)])
                            for e, hidden in enumerate((m.H0, m.H1, m.A3, m.B2)):
                                for k in range(2):
                                    last = pe.matmul(to[:, e * OUTW:(e + 1) * OUTW], hidden[:, k, t * P:(t + 1) * P],
                                                     wcol(f"d{e}", k * D + KEEP0, (k + 1) * D), start=(k == 0), stop=(k == 1))
                            last.then_inc(sm["t_work"], 1)

                @block.scalar
                def _(act):
                    def copy_work(s, to, scale=1.0, view=None):
                        act.wait_ge(sm["t_work"], nth_work[s])
                        src = ring_bank(s) if view is None else view(ring_bank(s))
                        act.activation(to, src, ACT.Copy, scale=scale).then_inc(sm["s_work"], 1)

                    act.activation(EPS[:, 3:4], EPS[:, 2:3], ACT.Exp)
                    for s in steps:
                        m = tiles_of(s)
                        if s[0] == "score":
                            _, g, j, (kt, half, lo, hi) = s
                            nth = nth_value[("values", g, s[3])]
                            if nth > PIECES:
                                act.wait_ge(sm["t_values"], nth - PIECES)
                            act.wait_ge(sm["t_scores"], nth_score[s])
                            act.activation(exps(s)[:, j, lo - half * BANK:hi - half * BANK], ring_bank(s)[:, 0:hi - lo], ACT.Exp)\
                               .then_inc(sm["s_exp"], 1)
                        elif s[0] == "evac":
                            g = s[1]
                            act.wait_ge(sm["t_values"], nth_value[("values", g, pcs[-1])])
                            for h in range(HALVES):
                                if g > 0:
                                    act.wait_ge(sm["t_ring"], nth_ring[("out", g - 1, h)])
                                act.activation(OT[:, half_cols(h)], bank(h), ACT.Copy).then_inc(sm["s_evac"], 1)
                        elif s[0] == "p_turn":
                            if s[1]:
                                act.wait_ge(sm["t_work"], nth_work[("p_v", s[1] - 1)])
                            copy_work(s, hT[:, :])
                        elif s[0] == "p_qk":
                            _, h, w = s
                            if h:
                                act.wait_ge(sm["g_parts"], nth_split[("p_split", h - 1, w, 1)])
                            copy_work(s, QK[:, w, :], scale=(SCALE if w == 0 and not prepared else 1.0))
                        elif s[0] == "p_v":
                            if attn is not None:
                                act.wait_ge(sm["g_vcopy"], 1)
                            copy_work(s, VS[:, 4 * s[1]:4 * s[1] + 4, :].rearrange("p t d -> p (t d)"))
                        elif s[0] == "p_root":
                            act.wait_ge(sm["v_root"], s[1] + 1)
                            act.activation(SQ[:, :, :].rearrange("p w (t a d q) -> p (w t a) d q", t=4, d=HD, q=2),
                                           ROOT[:, :, :, :].rearrange("p w t (a q) -> p (w t a) q", q=2).unsqueeze(2)
                                           .to_broadcast([P, 4 * H, HD, 2]), ACT.Sqrt).then_inc(sm["s_root"], 1)
                        elif s[0] == "p_split" and s[3] % 2 == 0:
                            _, h, w, n = s
                            if n:
                                act.wait_ge(sm["g_parts"], nth_split[("p_split", h, w, 1)])
                            elif prepared:
                                act.wait_ge(sm["v_work"], nth_vector[("p_spread", h, w)])
                            else:
                                act.wait_ge(sm["s_work"], nth_scalar[("p_qk", h, w)])
                            if h and n == 0:
                                act.wait_ge(sm[f"d_scratch{w}"], 16 * h)
                            act.activation(PARTS[:, w, n // 2, :], (SQ if n else QK)[:, w, :], ACT.Copy)\
                               .then_inc(sm["s_split"], 1)
                        elif s[0] == "m_aturn":
                            copy_work(s, AOT[:, half_cols(s[1])])
                        elif s[0] == "m_yturn":
                            if s[1] and not apart:
                                act.wait_ge(sm["t_work"], nth_work[("m_up", s[1] - 1, "e1u", 1)])
                            copy_work(s, m.YT)
                        elif s[0] == "m_rexp":
                            act.wait_ge(sm["v_logits"], nth_of_kind[("m_logits", s[1])])
                            act.activation(m.RT[:, 4, :, :], m.RT[:, 3, :, :], ACT.Exp).then_inc(sm["s_rexp"], 1)
                        elif s[0] == "m_up" and s[2] == "e1g":
                            _, c, name, chunk = s
                            act.wait_ge(sm["t_work"], nth_work[s])
                            if c and not apart:
                                act.wait_ge(sm["t_work"], nth_work[("m_down", c - 1, 3)])
                            act.activation(m.TH[:, chunk, :], ring_bank(s), ACT.Tanh, scale=0.5).then_inc(sm["s_tanh"], 1)
                        elif s[0] == "m_gelu":
                            _, c, level = s
                            newest = (("e3a", 0), ("e2b", 1), ("e2c", 1))[level]
                            act.wait_ge(sm["v_work"], nth_vector[("m_up", c) + newest])
                            act.activation(m.LEVELS[level], m.LEVELS[level], ACT.Gelu).then_inc(sm["s_gelu"], 1)

                @block.vector
                def _(dve):
                    chain = [0]

                    def link(ins):
                        chain[0] += 1
                        ins.then_inc(sm["v_chain"], 1)
                        dve.wait_ge(sm["v_chain"], chain[0])

                    def wide(small):
                        return small.unsqueeze(2).to_broadcast([P, 4, E])

                    if apart:
                        link(dve.memset(second_tiles.CMP, 0.0))

                    def x_cols(b, c):
                        return X[:, bass.ts(b * HALVES + c, BANK)]

                    for s in steps:
                        m = tiles_of(s)
                        if s[0] == "max":
                            _, g, j, qt, lo, hi = s
                            if g > 1 and ("split", g - 1) in steps:
                                dve.wait_ge(sm["g_split"], turns.index(("turn", g - 1)) + 1)
                            dve.wait_ge(sm["t_ring"], nth_ring[s])
                            dve.tensor_reduce(NM[:, lo // BANK, qt, j:j + 1], ring_bank(s)[:, 0:hi - lo], AXX, ALU.max,
                                              negate=True).then_inc(sm["v_ring"], 1)
                        elif s[0] == "split":
                            dve.wait_ge(sm["v_ring"], last_max[s[1]])
                            both = slice(4 if kind[s[1]] else 0, T)
                            dve.tensor_tensor(NM[:, 0, both, :], NM[:, 0, both, :], NM[:, 1, both, :], ALU.min)\
                               .then_inc(sm["v_max"], 1)
                        elif s[0] == "turn":
                            n = turns.index(s)
                            if n:
                                dve.wait_ge(sm["d_max"], 64 * n)
                            dve.wait_ge(sm["t_ring"], nth_ring[s])
                            dve.tensor_copy(CTS[:, :], ring_bank(s).bitcast(BF16)[0:4 * NC_ROWS, 0:S])\
                               .then_inc(sm["v_ring"], 1)
                        elif s[0] == "out":
                            _, g, h = s
                            dve.wait_ge(sm["t_ring"], nth_ring[s])
                            if g == 0 and finished is not None:
                                dve.wait_ge(sm["t_work"], nth_work[("m_aturn", h)])
                            o = ring_bank(s).rearrange("p (t j c) -> p t j c", t=4, j=4)
                            if g > 0:
                                dve.wait_ge(sm["v_ring"], nth_ring[("out", g - 1, h)])
                            tiles = slice(4 * h, 4 * h + 4)
                            link(dve.reciprocal(RD[:, tiles, :], o[:, :, :, HD]))
                            dve.tensor_tensor(AO[:, tiles, 32 * g:32 * (g + 1)].rearrange("p t (j d) -> p t j d", j=4),
                                              o[:, :, :, 0:HD], RD[:, tiles, :].unsqueeze(3).to_broadcast([P, 4, 4, HD]),
                                              ALU.mult).then_inc(sm["v_ring"], 1)
                        elif s[0] == "p_stats":
                            for t in range(T):
                                last = dve.bn_stats(BST[:, t, :], X[:, bass.ts(b_prep * T + t, D)])
                            link(last)
                            for t in range(T):
                                last = dve.bn_aggr(MV[:, t, :], BST[:, t, :])
                            last.then_inc(sm["v_stats"], 1)
                            dve.wait_ge(sm["v_stats"], 1)
                            dve.tensor_copy(MVA[:, bass.ts(b_prep, 2 * T)], MV[:, :, :].rearrange("p t n -> p (t n)"))
                        elif s[0] == "p_norm":
                            h = s[1]
                            dve.wait_ge(sm["g_rr"], 1)
                            if h:
                                dve.wait_ge(sm["t_work"], nth_work[("p_turn", h - 1)])
                            for t in range(4):
                                tile = 4 * h + t
                                last = dve.tensor_scalar(HN[:, t, :], X[:, bass.ts(b_prep * T + tile, D)], MV[:, tile, 0:1],
                                                         RR[:, tile:tile + 1], ALU.subtract, ALU.mult)
                            last.then_inc(sm["v_norm"], 1)
                        elif s[0] == "p_sum":
                            dve.wait_ge(sm["t_work"], nth_work[s])
                            if s[1]:
                                dve.wait_ge(sm["s_root"], s[1])
                            dve.tensor_scalar(ROOT[:, :, :, :].rearrange("p w t h -> p (w t h)"),
                                              ring_bank(s)[:, 0:2 * 4 * H], 1.0 / HD, RMS_EPS, ALU.mult, ALU.add)\
                               .then_inc(sm["v_work"], 1)
                            dve.wait_ge(sm["v_work"], nth_vector[s])
                            dve.reciprocal(ROOT[:, :, :, :], ROOT[:, :, :, :]).then_inc(sm["v_root"], 1)
                        elif s[0] == "p_spread":
                            _, h, w = s
                            dve.wait_ge(sm["t_work"], nth_work[s])
                            dve.scalar_tensor_tensor(QK[:, w, :], QK[:, w, :], VEC[:, 2 + w:3 + w], ring_bank(s),
                                                     ALU.mult, ALU.mult).then_inc(sm["v_work"], 1)
                        elif s[0] == "m_out":
                            dve.wait_ge(sm["t_work"], nth_work[s])
                            rows = x_cols(b_done, s[1])
                            dve.tensor_tensor(rows, rows, ring_bank(s), ALU.add).then_inc(sm["v_work"], 1)
                        elif s[0] == "m_u":
                            c = s[1]
                            if c and not apart:
                                dve.wait_ge(sm["v_x"], c)
                            for t in range(4):
                                tile = 4 * c + t
                                last = dve.tensor_scalar(m.UM[:, t, :], X[:, bass.ts(b_done * T + tile, D)],
                                                         MVA[:, bass.ds(b_done * (2 * T) + 2 * tile, 1)],
                                                         RSTDA[:, bass.ds(b_done * T + tile, 1)], ALU.subtract, ALU.mult)
                            link(last)
                        elif s[0] == "m_ao":
                            dve.wait_ge(sm["t_work"], nth_work[s])
                            kept = m.UM[:, :, KEEP0:D]
                            dve.tensor_tensor(kept, kept, ring_bank(s)[:, 0:4 * OUTW].rearrange("p (t n) -> p t n", t=4),
                                              ALU.add).then_inc(sm["v_work"], 1)
                        elif s[0] == "m_rms":
                            dve.wait_ge(sm["g_msquare"], nth_of_kind[("m_square", s[1])])
                            dve.tensor_reduce(m.R2[:, :], m.YN[:, :, :], AXX, ALU.add).then_inc(sm["v_sums"], 1)
                        elif s[0] == "m_gate":
                            dve.wait_ge(sm["t_work"], nth_work[s])
                            dve.tensor_copy(m.RT[:, 0, :, :], ring_bank(s)[:, 0:4 * E].rearrange("p (t e) -> p t e", t=4))\
                               .then_inc(sm["v_work"], 1)
                        elif s[0] == "m_logits":
                            dve.wait_ge(sm["v_work"], nth_vector[("m_gate", s[1])])
                            dve.memset(m.RT[:, 1, :, :], 0.0)
                            link(dve.tensor_tensor(m.RT[:, 2, :, :].bitcast(I32), m.RT[:, 0, :, :], m.RT[:, 0, :, :], ALU.is_equal))
                            link(dve.copy_predicated(m.RT[:, 1, :, :], m.RT[:, 2, :, :].bitcast(I32), m.RT[:, 0, :, :]))
                            link(dve.tensor_scalar(m.RT[:, 1, :, :], m.RT[:, 1, :, :], FMAX, -FMAX, ALU.min, ALU.max))
                            link(dve.tensor_reduce(m.RS[:, 0, :], m.RT[:, 1, :, :], AXX, ALU.max))
                            dve.tensor_tensor(m.RT[:, 3, :, :], m.RT[:, 1, :, :], wide(m.RS[:, 0, :]), ALU.subtract)\
                               .then_inc(sm["v_logits"], 1)
                        elif s[0] == "m_route":
                            dve.wait_ge(sm["s_rexp"], nth_of_kind[("m_rexp", s[1])])
                            link(dve.tensor_reduce(m.RS[:, 1, :], m.RT[:, 4, :, :], AXX, ALU.add))
                            link(dve.reciprocal(m.RS[:, 1, :], m.RS[:, 1, :]))
                            link(dve.tensor_tensor(m.RT[:, 5, :, :], m.RT[:, 4, :, :], wide(m.RS[:, 1, :]), ALU.mult))
                            for j in range(E):
                                for lo, hi, op in ((0, j, ALU.is_gt), (j + 1, E, ALU.is_ge)):
                                    if lo < hi:
                                        last = dve.tensor_tensor(m.CMP[:, :, lo:hi, j],
                                                                 m.RT[:, 5, :, j:j + 1].to_broadcast([P, 4, hi - lo]),
                                                                 m.RT[:, 5, :, lo:hi], op)
                            link(last)
                            link(dve.tensor_reduce(m.RT[:, 6, :, :], m.CMP[:, :, :, :], AXX, ALU.add))
                            link(dve.scalar_tensor_tensor(m.RT[:, 8, :, :], m.RT[:, 6, :, :], 2.0, m.RT[:, 5, :, :],
                                                          ALU.is_lt, ALU.mult))
                            link(dve.tensor_reduce(m.RS[:, 2, :], m.RT[:, 8, :, :], AXX, ALU.add))
                            link(dve.tensor_scalar(m.RS[:, 2, :], m.RS[:, 2, :], 1e-8, None, ALU.add))
                            link(dve.reciprocal(m.RS[:, 2, :], m.RS[:, 2, :]))
                            link(dve.tensor_tensor(m.RT[:, 9, :, :], m.RT[:, 8, :, :], wide(m.RS[:, 2, :]), ALU.mult))
                        elif s[0] == "m_up":
                            _, c, name, chunk = s
                            if c and not apart and (name, chunk) in (("e0u", 0), ("e1g", 0)):
                                dve.wait_ge(sm["t_work"], nth_work[("m_down", c - 1, 3)])
                            if name == "e1g":
                                dve.wait_ge(sm["s_tanh"], nth_tanh[s])
                                dve.scalar_tensor_tensor(m.TH[:, chunk, :], m.TH[:, chunk, :], 1.0, ring_bank(s),
                                                         ALU.add, ALU.mult).then_inc(sm["v_work"], 1)
                            elif name == "e1u":
                                dve.wait_ge(sm["v_work"], nth_vector[("m_up", c, "e1g", chunk)])
                                dve.wait_ge(sm["t_work"], nth_work[s])
                                dve.scalar_tensor_tensor(m.H1[:, chunk, :], m.TH[:, chunk, :], 0.5, ring_bank(s),
                                                         ALU.mult, ALU.mult).then_inc(sm["v_work"], 1)
                            else:
                                if name == "e3b":
                                    dve.wait_ge(sm["v_work"], nth_vector[("m_up", c, "e1u", chunk)])
                                dve.wait_ge(sm["t_work"], nth_work[s])
                                raw = {"e0u": m.H0, "e2a": m.A1, "e3a": m.B1, "e3b": m.B2, "e2b": m.A2, "e2c": m.A3}[name]
                                dve.tensor_copy(raw[:, chunk, :], ring_bank(s)).then_inc(sm["v_work"], 1)
                        elif s[0] == "m_down":
                            _, c, t = s
                            dve.wait_ge(sm["t_work"], nth_work[s])
                            dve.tensor_tensor(WD[:, t % 2, :, :],
                                              ring_bank(s)[:, 0:E * OUTW].rearrange("p (e n) -> p e n", e=E),
                                              m.RT[:, 9, t, :].unsqueeze(2).to_broadcast([P, E, OUTW]), ALU.mult)\
                               .then_inc(sm["v_work"], 1)
                            dve.wait_ge(sm["v_work"], nth_vector[s])
                            link(dve.tensor_reduce(WS[:, t % 2, :], WD[:, t % 2, :, :].rearrange("p e n -> p n e"),
                                                   AXX, ALU.add))
                            link(dve.tensor_tensor(m.UM[:, t, KEEP0:D], m.UM[:, t, KEEP0:D], WS[:, t % 2, :], ALU.add))
                        elif s[0] == "m_x":
                            rows = x_cols(b_done, s[1])
                            dve.scalar_tensor_tensor(rows, m.UM[:, :, :].rearrange("p t d -> p (t d)"), 0.5, rows,
                                                     ALU.mult, ALU.add).then_inc(sm["v_x"], 1)

                    if first:
                        dve.wait_ge(loaded_late, 16 * 2)
                        late = W[:, WAT["gate"]:WAT["wo"]]
                        dve.tensor_scalar(late, late, VEC[:, 1:2], None, ALU.mult)

                @block.gpsimd
                def _(pool):
                    chain = [0]

                    def link(ins):
                        chain[0] += 1
                        ins.then_inc(sm["g_chain"], 1)
                        pool.wait_ge(sm["g_chain"], chain[0])

                    def minus_half(n):
                        return EPS[:, 4:5].to_broadcast([P, n])

                    for s in steps:
                        m = tiles_of(s)
                        if s[0] == "score" and diagonal(s[3]):
                            _, g, j, (kt, half, lo, hi) = s
                            pool.wait_ge(sm["s_exp"], nth_score[s])
                            tile = exps(s)[:, j, lo - half * BANK:lo - half * BANK + P]
                            pool.affine_select(out=tile, in_=tile, compare_op=ALU.is_ge, fill=0.0, base=0,
                                               pattern=[[1, P]], channel_multiplier=-1).then_inc(sm["g_diag"], 1)
                        elif s[0] == "split":
                            g = s[1]
                            pool.wait_ge(sm["v_max"], turns.index(("turn", g)) + 1)
                            if turns.index(("turn", g)):
                                pool.wait_ge(sm["t_ring"], nth_ring[turns[turns.index(("turn", g)) - 1]])
                            link(pool.tensor_copy(CT[:, :, 0, :], NM[:, 0, :, :]))
                            link(pool.tensor_tensor(NR[:, :, :], NM[:, 0, :, :], CT[:, :, 0, :], ALU.subtract))
                            link(pool.tensor_copy(CT[:, :, 1, :], NR[:, :, :]))
                            pool.tensor_tensor(CT[:, :, 2, :], NR[:, :, :], CT[:, :, 1, :], ALU.subtract)\
                                .then_inc(sm["g_split"], 1)
                            pool.wait_ge(sm["g_split"], turns.index(("turn", g)) + 1)
                        elif s[0] == "v_copy":
                            g = s[1]
                            if g >= G:
                                pool.wait_ge(sm["s_work"], nth_scalar[("p_v", 1)])
                                if attn is not None:
                                    pool.wait_ge(sm["t_values"], nth_value[("values", g - G, pcs[-1])])
                            h0 = 4 * (g % G)
                            pool.tensor_copy(V[:, :, h0:h0 + 4, 0:HD],
                                             VS[:, :, h0 * HD:(h0 + 4) * HD].rearrange("p t (j d) -> p t j d", j=4))\
                                .then_inc(sm["g_vcopy"], 1)
                        elif s[0] == "p_stats":
                            pool.wait_ge(sm["v_stats"], 1)
                            link(pool.tensor_scalar(RR[:, :], MV[:, :, 1], LN_EPS, None, ALU.add))
                            link(pool.tensor_tensor(RSTD[:, :], RR[:, :], minus_half(T), ALU.pow))
                            if prepared:
                                link(pool.tensor_tensor(RR[:, :], MV[:, :, 1], RSTD[:, :], ALU.mult))
                                link(pool.tensor_tensor(RR[:, :], RR[:, :], RSTD[:, :], ALU.mult))
                                link(pool.tensor_scalar(RR[:, :], RR[:, :], RMS_EPS, None, ALU.add))
                                link(pool.tensor_tensor(RR[:, :], RR[:, :], minus_half(T), ALU.pow))
                                pool.tensor_tensor(RR[:, :], RR[:, :], RSTD[:, :], ALU.mult).then_inc(sm["g_rr"], 1)
                            else:
                                pool.tensor_copy(RR[:, :], RSTD[:, :]).then_inc(sm["g_rr"], 1)
                            pool.tensor_copy(RSTDA[:, bass.ts(b_prep, T)], RSTD[:, :])
                        elif s[0] == "p_square":
                            _, h, w = s
                            pool.wait_ge(sm["s_work"], nth_scalar[("p_qk", h, w)])
                            if h:
                                pool.wait_ge(sm["g_parts"], nth_split[("p_split", h - 1, w, 3)])
                            pool.tensor_tensor(SQ[:, w, :], QK[:, w, :], QK[:, w, :], ALU.mult).then_inc(sm["g_square"], 1)
                        elif s[0] == "p_split" and s[3] % 2:
                            _, h, w, n = s
                            former = QK[:, w, :] if n == 1 else SQ[:, w, :]
                            pool.wait_ge(sm["s_split"], nth_split[("p_split", h, w, n - 1)])
                            if h and n == 1:
                                pool.wait_ge(sm["g_parts"], nth_split[("p_split", h - 1, w, 3)])
                            pool.tensor_tensor(SQ[:, w, :] if n == 1 else PARTS[:, w, 2, :], former,
                                               PARTS[:, w, n // 2, :], ALU.subtract).then_inc(sm["g_parts"], 1)
                        elif s[0] == "m_square":
                            c = s[1]
                            pool.wait_ge(sm["v_work"], nth_vector[("m_ao", c)])
                            if c and not apart:
                                pool.wait_ge(sm["t_work"], nth_work[("m_yturn", c - 1)])
                            pool.tensor_tensor(m.YN[:, :, :], m.UM[:, :, :], m.UM[:, :, :], ALU.mult).then_inc(sm["g_msquare"], 1)
                        elif s[0] == "m_norm":
                            c = s[1]
                            pool.wait_ge(sm["v_sums"], nth_of_kind[("m_rms", c)])
                            link(pool.tensor_scalar(m.R2[:, :], m.R2[:, :], 1.0 / D, RMS_EPS, ALU.mult, ALU.add))
                            pool.tensor_tensor(m.R2[:, :], m.R2[:, :], minus_half(4), ALU.pow).then_inc(sm["g_norm"], 1)
                            pool.wait_ge(sm["g_norm"], 2 * nth_of_kind[s] - 1)
                            pool.tensor_tensor(m.YN[:, :, :], m.UM[:, :, :], m.R2[:, :].unsqueeze(2).to_broadcast([P, 4, D]),
                                               ALU.mult).then_inc(sm["g_norm"], 1)

                @block.sync
                def _(sp):
                    for s in steps:
                        m = tiles_of(s)
                        if s[0] == "stack":
                            g = s[1]
                            now = attn if g < G else prepared
                            if g >= G:
                                for w in range(2):
                                    sp.wait_ge(sm[f"d_scratch{w}"], 16 * HALVES)
                                if attn is not None:
                                    sp.wait_ge(sm["t_scores"], nth_score[("score", g - G, 3, pcs[-1])])
                            stacked, g = sm[f"d_stack{g}"], g % G
                            scr = SCR.rearrange("w s (g e d q) t -> w g e s d (q t)", g=G, e=2, d=HD)
                            for e in range(2):
                                qs = QS[:, 2 * g:2 * g + 2, :].rearrange("p q t -> p (q t)")
                                kz = KZ[:, e, 2 * g:2 * g + 2, :].rearrange("p q t -> p (q t)")
                                sp.dma_start(QS[HROWS * e + EXTRA:HROWS * (e + 1), 2 * g:2 * g + 2, :],
                                             query_rows[0 if now else 1].rearrange("r (g q e) t -> g e r q t", g=G, e=2)
                                             [g, e]).then_inc(stacked, 16)
                                at = HROWS * e
                                for part, n in ((0, 3), (1, 2), (2, 1)):
                                    sp.dma_start(qs[at:at + n * HD],
                                                 scr[0, g, e, part].unsqueeze(0).to_broadcast([n, HD, 2 * S]))\
                                      .then_inc(stacked, 16)
                                    at += n * HD
                                at = HROWS * e
                                for n in (3, 2, 1):
                                    sp.dma_start(kz[at:at + n * HD], scr[1, g, e, 0:n])\
                                      .then_inc(stacked, 16)
                                    at += n * HD
                        elif s[0] == "p_store":
                            _, h, w = s
                            if attn is not None:
                                sp.wait_ge(sm["d_stack3"], STACKED)
                            sp.wait_ge(sm["g_parts"], nth_split[("p_split", h, w, 3)])
                            sp.dma_start(SCR[w].rearrange("s p t -> p s t")[:, :, half_cols(h)], PARTS[:, w, :, :])\
                              .then_inc(sm[f"d_scratch{w}"], 16)
                        elif s[0] == "turn":
                            g = s[1] % G
                            sp.wait_ge(sm["v_ring"], nth_ring[s])
                            for j in range(4):
                                row = HROWS * (j % 2) + EXTRA
                                sp.dma_start(QS[row:row + NC_ROWS, 2 * g + j // 2, :], CTS[j:4 * NC_ROWS:4, :])\
                                  .then_inc(sm["d_max"], 16)
                        elif s[0] == "m_x" and store:
                            c = s[1]
                            sp.wait_ge(sm["v_x"], nth_of_kind[s])
                            sp.dma_start(out.rearrange("b (t p) d -> p (b t) d", p=P)[:, bass.ts(b_done * HALVES + c, 4), :],
                                         X[:, bass.ts(b_done * HALVES + c, BANK)].rearrange("p (t d) -> p t d", t=4))\
                              .then_inc(sm["d_out"], 16)
                    if first:
                        sp.wait_ge(loaded_late, 16 * 2)
                    for s in stacks:
                        sp.wait_ge(sm[f"d_stack{s[1]}"], STACKED)
                    if turns:
                        sp.wait_ge(sm["d_max"], 64 * len(turns))
                    if store and finished is not None:
                        sp.wait_ge(sm["d_out"], 16 * HALVES)

            clear(sm)

        slot(None, None, prepared=True, b_prep=0, first=True)
        for layer, ffn in enumerate((True, False, True)):
            before, after = (None, True, False)[layer], (False, True, None)[layer]
            last_layer = after is None
            slot(ffn, 0, prepared=ffn, b_prep=1, finished=before, b_done=B - 1)
            with nc.Fori(1, B - 1) as b:
                slot(ffn, b, prepared=ffn, b_prep=b + 1, finished=ffn, b_done=b - 1, store=last_layer)
            slot(ffn, B - 1, prepared=after, b_prep=0, finished=ffn, b_done=B - 2, store=last_layer)
        slot(None, None, finished=True, b_done=B - 1, store=True)


def kernel(**inputs):
    import numpy as _np
    import concourse.bacc as _bacc
    from concourse import mybir as _mybir
    from concourse.bass_utils import run_bass_kernel_spmd as _run

    a = {k: _np.asarray(v) for k, v in inputs.items()}

    def up(name):
        return a["L0_ffn_" + name].T

    def two(w):
        return _np.concatenate([w[:P], w[P:]], axis=1)

    def per_head(w):
        return _np.repeat(w.reshape(D, KV, HD), H // KV, axis=1).reshape(D, H * HD)

    at = {"wq": up("wq")[:, ROW_FEATURE], "wk": up("wk")[:, ROW_FEATURE], "wv": up("wv"), "gate": up("gate_w"), "e0u": up("e0_up"),
          "e1g": up("e1_w1"), "e1u": up("e1_w2"), "e2a": up("e2_l1"), "e3a": up("e3_down"), "wo": up("wo"),
          "e2b": two(up("e2_l2")), "e2c": two(up("e2_l3")), "e3b": up("e3_up"),
          "d0": two(up("e0_down")), "d1": two(up("e1_down")), "d2": two(up("e2_l4")), "d3": two(up("e3_out")),
          "aq": a["L0_attn_Wq"][:, ROW_FEATURE], "ak": per_head(a["L0_attn_Wk"])[:, ROW_FEATURE],
          "av": per_head(a["L0_attn_Wv"]), "ao": a["L0_attn_Wo"]}
    weights = _np.ascontiguousarray(_np.concatenate([at[name] for name, _ in WPARTS], axis=1))
    vectors = _np.ascontiguousarray(_np.stack([a["L0_ffn_n1_w"], a["L0_ffn_n2_w"], a["L0_ffn_qn_w"][ROW_FEATURE % HD],
                                               a["L0_ffn_kn_w"][ROW_FEATURE % HD]], axis=1))
    key, query = additive_rows()
    bf16 = _mybir.dt.np(_mybir.dt.bfloat16)
    key = _np.ascontiguousarray(_np.repeat(key[:, None, :], H // 2, axis=1)).astype(bf16)
    arrays = {"x": _np.ascontiguousarray(a["L0_attn_x"]), "weights": weights, "vectors": vectors,
              "head_of": (ROW_HEAD[:, None] == ROWS_HEADS).astype(_np.float32),
              "key_rows": key, "query_rows": query.astype(bf16)}

    nc = _bacc.Bacc("TRN2", target_bir_lowering=False, num_devices=1)
    args = [nc.dram_tensor(name, v.shape, _mybir.dt.from_np(v.dtype), kind="ExternalInput").ap()
            for name, v in arrays.items()]
    out = nc.dram_tensor("out", (B, S, D), FP32, kind="ExternalOutput").ap()
    macaron_kernel(nc, *args, out)
    r = _run(nc, [arrays], core_ids=[0])
    return r.results[0]["out"]
```
